# Optimizing a Trainium2 kernel written in Bass

```python
import numpy as np
import jax
import jax.numpy as jnp

def _softmax(x, axis=-1):
    return jax.nn.softmax(x, axis=axis)

def _gelu(x):
    return jax.nn.gelu(x, approximate=True)

def _silu(x):
    return jax.nn.silu(x)

def _sigmoid(x):
    return jax.nn.sigmoid(x)

def _layernorm(x, axis=-1, eps=1e-05):
    m = jnp.mean(x, axis=axis, keepdims=True)
    v = jnp.var(x, axis=axis, keepdims=True)
    return (x - m) / jnp.sqrt(v + eps)

def _scatter_add(tgt, idx, src, axis=0):
    return tgt.at[idx].add(src)

def _segment_sum(src, seg, n):
    return jax.ops.segment_sum(src, seg, n)
kernel_name = 'mk_sandwich_d1_jaxref_r8_552990'

def setup_inputs(seed: int=0):
    np.random.seed(seed)
    _w = jnp.asarray

    def _L0_attn_setup():
        import math
        import jax, jax.numpy as jnp
        import numpy as np
        NUM_HEADS = 8
        ATTN_STD = np.array([1.0, 2.0, 4.0, 8.0, 1.0, 2.0, 4.0, 8.0], dtype=np.float32)
        ATTN_OFFSET = np.array([-1.0, -2.0, -4.0, -8.0, -1.0, -2.0, -4.0, -8.0], dtype=np.float32)

        def _gaussian_attn_weights(qlen, dtype):
            stds = jnp.asarray(ATTN_STD, dtype=dtype)[:, None, None]
            offs = jnp.asarray(ATTN_OFFSET, dtype=dtype)[:, None, None]
            q = jnp.arange(qlen, dtype=dtype)[None, :, None]
            k = jnp.arange(qlen, dtype=dtype)[None, None, :]
            dist = k - q - offs
            inv_norm = 1.0 / (stds * math.sqrt(2.0 * math.pi))
            return inv_norm * jnp.exp(-0.5 * (dist / stds) ** 2)
        key = jax.random.key(seed)
        k1, k2, k3 = jax.random.split(key, 3)
        B, L, D = (2, 256, 128)
        values = jax.random.normal(k1, (B, L, D), dtype=jnp.float32)
        input_weights = 0.02 * jax.random.normal(k2, (D, D), dtype=jnp.float32)
        output_weight = 0.02 * jax.random.normal(k3, (D, D), dtype=jnp.float32)
        return {'values': values, 'input_weights': input_weights, 'output_weight': output_weight}
    _L0_attn_in = _L0_attn_setup()

    def _L0_ffn_setup():
        import jax, jax.numpy as jnp
        import numpy as np
        E = 8
        D = 128
        F = 512
        S, B = (256, 2)
        LN_EPS = 1e-05

        def _moe_forward(input_features, centroids, ln_g, ln_b, W1, b1, W2, b2):
            s, b, d = input_features.shape
            x = jnp.swapaxes(input_features, 0, 1).reshape(-1, d)
            logits = x.astype(jnp.float32) @ centroids.astype(jnp.float32).T
            assign = jnp.argmax(logits, axis=-1)
            onehot = jax.nn.one_hot(assign, E, dtype=x.dtype)
            disp = jnp.einsum('te,td->etd', onehot, x)
            mu = disp.mean(-1, keepdims=True)
            var = disp.var(-1, keepdims=True)
            xn = (disp - mu) * jax.lax.rsqrt(var + LN_EPS)
            xn = xn * ln_g[:, None, :] + ln_b[:, None, :]
            h = jax.nn.relu(jnp.einsum('etd,edf->etf', xn, W1) + b1[:, None, :])
            y = jnp.einsum('etf,efd->etd', h, W2) + b2[:, None, :]
            y = disp + y
            out = jnp.einsum('te,etd->td', onehot, y)
            return jnp.swapaxes(out.reshape(b, s, d), 0, 1)
        key = jax.random.key(seed)
        ks = jax.random.split(key, 8)
        scale_in = 1.0 / np.sqrt(D)
        scale_ff = 1.0 / np.sqrt(F)
        return {'input_features': jax.random.normal(ks[0], (S, B, D), dtype=jnp.float32), 'centroids': jax.random.normal(ks[1], (E, D), dtype=jnp.float32) * scale_in, 'ln_g': jnp.ones((E, D), dtype=jnp.float32), 'ln_b': jnp.zeros((E, D), dtype=jnp.float32), 'W1': jax.random.normal(ks[2], (E, D, F), dtype=jnp.float32) * scale_in, 'b1': jax.random.normal(ks[3], (E, F), dtype=jnp.float32) * 0.01, 'W2': jax.random.normal(ks[4], (E, F, D), dtype=jnp.float32) * scale_ff, 'b2': jax.random.normal(ks[5], (E, D), dtype=jnp.float32) * 0.01}
    _L0_ffn_in = _L0_ffn_setup()
    _d = {'L0_attn_values': _L0_attn_in['values'], 'L0_attn_input_weights': _L0_attn_in['input_weights'], 'L0_attn_output_weight': _L0_attn_in['output_weight'], 'L0_ffn_centroids': _L0_ffn_in['centroids'], 'L0_ffn_ln_g': _L0_ffn_in['ln_g'], 'L0_ffn_ln_b': _L0_ffn_in['ln_b'], 'L0_ffn_W1': _L0_ffn_in['W1'], 'L0_ffn_b1': _L0_ffn_in['b1'], 'L0_ffn_W2': _L0_ffn_in['W2'], 'L0_ffn_b2': _L0_ffn_in['b2']}
    _x0 = _d['L0_attn_values']
    _d['L0_attn_values'] = jax.random.normal(jax.random.fold_in(jax.random.key(seed), 1), (8, 256, 128), dtype=_x0.dtype)
    del _x0
    return _d

def reference(L0_attn_values, L0_attn_input_weights, L0_attn_output_weight, L0_ffn_centroids, L0_ffn_ln_g, L0_ffn_ln_b, L0_ffn_W1, L0_ffn_b1, L0_ffn_W2, L0_ffn_b2):

    def _L0_attn_ref(values, input_weights, output_weight):
        import math
        import jax, jax.numpy as jnp
        import numpy as np
        NUM_HEADS = 8
        ATTN_STD = np.array([1.0, 2.0, 4.0, 8.0, 1.0, 2.0, 4.0, 8.0], dtype=np.float32)
        ATTN_OFFSET = np.array([-1.0, -2.0, -4.0, -8.0, -1.0, -2.0, -4.0, -8.0], dtype=np.float32)

        def _gaussian_attn_weights(qlen, dtype):
            stds = jnp.asarray(ATTN_STD, dtype=dtype)[:, None, None]
            offs = jnp.asarray(ATTN_OFFSET, dtype=dtype)[:, None, None]
            q = jnp.arange(qlen, dtype=dtype)[None, :, None]
            k = jnp.arange(qlen, dtype=dtype)[None, None, :]
            dist = k - q - offs
            inv_norm = 1.0 / (stds * math.sqrt(2.0 * math.pi))
            return inv_norm * jnp.exp(-0.5 * (dist / stds) ** 2)
        B, L, D = values.shape
        H = NUM_HEADS
        pd = D // H
        v = values @ input_weights.T
        v = v.reshape(B, L, H, pd).transpose(0, 2, 1, 3)
        probs = _gaussian_attn_weights(L, values.dtype)
        attended = jnp.einsum('hqk,bhkd->bhqd', probs, v)
        attended = attended.transpose(0, 2, 1, 3).reshape(B, L, D)
        return attended @ output_weight.T

    def _L0_ffn_ref(input_features, centroids, ln_g, ln_b, W1, b1, W2, b2):
        import jax, jax.numpy as jnp
        import numpy as np
        E = 8
        D = 128
        F = 512
        S, B = (256, 2)
        LN_EPS = 1e-05

        def _moe_forward(input_features, centroids, ln_g, ln_b, W1, b1, W2, b2):
            s, b, d = input_features.shape
            x = jnp.swapaxes(input_features, 0, 1).reshape(-1, d)
            logits = x.astype(jnp.float32) @ centroids.astype(jnp.float32).T
            assign = jnp.argmax(logits, axis=-1)
            onehot = jax.nn.one_hot(assign, E, dtype=x.dtype)
            disp = jnp.einsum('te,td->etd', onehot, x)
            mu = disp.mean(-1, keepdims=True)
            var = disp.var(-1, keepdims=True)
            xn = (disp - mu) * jax.lax.rsqrt(var + LN_EPS)
            xn = xn * ln_g[:, None, :] + ln_b[:, None, :]
            h = jax.nn.relu(jnp.einsum('etd,edf->etf', xn, W1) + b1[:, None, :])
            y = jnp.einsum('etf,efd->etd', h, W2) + b2[:, None, :]
            y = disp + y
            out = jnp.einsum('te,etd->td', onehot, y)
            return jnp.swapaxes(out.reshape(b, s, d), 0, 1)
        return _moe_forward(input_features, centroids, ln_g, ln_b, W1, b1, W2, b2)
    x = L0_attn_values
    x = x + _layernorm(_L0_attn_ref(_layernorm(x, axis=-1), L0_attn_input_weights, L0_attn_output_weight), axis=-1)
    x = x + _layernorm(_L0_ffn_ref(_layernorm(x, axis=-1), L0_ffn_centroids, L0_ffn_ln_g, L0_ffn_ln_b, L0_ffn_W1, L0_ffn_b1, L0_ffn_W2, L0_ffn_b2), axis=-1)
    return x

_drawn_inputs = setup_inputs


def setup_inputs(seed=0):
    import zlib

    import numpy as np

    out = dict(_drawn_inputs(seed))
    spreads = {'L0_ffn_ln_g': (1.0, 0.2), 'L0_ffn_ln_b': (0.0, 0.324)}
    factors = {'L0_ffn_b1': 22.954, 'L0_ffn_b2': 8.0}
    for name, (base, spread) in spreads.items():
        noise = np.random.default_rng([zlib.crc32(name.encode()), seed]).standard_normal(out[name].shape)
        drawn = base * np.exp(spread * noise) if base else spread * noise
        out[name] = jnp.asarray(drawn.astype(out[name].dtype))
    for name, factor in factors.items():
        out[name] = (out[name] * factor).astype(out[name].dtype)
    return out
```

```python
import concourse.bass as bass
from concourse import mybir
from contextlib import ExitStack

ATTN_STD = (1.0, 2.0, 4.0, 8.0)
ATTN_OFFSET = (-1.0, -2.0, -4.0, -8.0)


def attention_moe_block(nc, x_d, wi_d, wo_d, cent_d, lng_d, lnb_d, w1_d, b1_d, w2_d, b2_d, toep_d, out_d):
    fp32, bf16, f16, i32 = mybir.dt.float32, mybir.dt.bfloat16, mybir.dt.float16, mybir.dt.int32
    u32 = mybir.dt.uint32
    ALU, ACT, AX = mybir.AluOpType, mybir.ActivationFunctionType, mybir.AxisListType

    P = 128
    B, L, D = x_d.shape
    E, _, F = w1_d.shape
    T = B * L
    NT = T // P
    FB = F // P
    CAP = NT + E - 1
    NG = len(ATTN_STD)
    HD = D // (2 * NG)
    HALF = NT // 2
    NB = HALF // 2
    EPS = 1e-5
    S = 64.0
    ROW = D + 2
    CE = D + E
    NR = 2 * E + E + FB * E

    x1_dram = nc.dram_tensor("x1_rows", [T, ROW], fp32, kind="Internal").ap()
    x1_view = x1_dram.rearrange("(t p) c -> p t c", p=P)
    x_view = x_d.rearrange("b l d -> (b l) d").rearrange("(t p) d -> p t d", p=P)
    out_rows = out_d.rearrange("b l d -> (b l) d")

    ctx = ExitStack()
    with ctx:
        def sb(name, shape, dt=fp32):
            return ctx.enter_context(nc.sbuf_tensor(name, shape, dt))

        def sem(name):
            return ctx.enter_context(nc.semaphore(name))

        bank = [ctx.enter_context(nc.psum_tensor(f"bank{i}", [P, 512], fp32)) for i in range(8)]

        ident = sb("ident", [P, P])
        ones_bf = sb("ones_bf", [P, P], bf16)
        before = sb("before", [P, P], bf16)
        lane = sb("lane", [P, P], bf16)
        tile_no = sb("tile_no", [P, CAP + 1])
        tile_thr = sb("tile_thr", [P, NT])
        first_wt = sb("first_wt", [P, E])
        lane_col = sb("lane_col", [P, 1])
        ones_e = sb("ones_e", [P, E])
        eps_t = sb("eps_t", [P, 1])
        small = sb("small", [NR, D])
        smallT = sb("smallT", [P, NR])
        wi = sb("wi", [P, D])
        wo = sb("wo", [P, D])
        wxc = sb("wxc", [P, CE])
        woc = sb("woc", [P, CE])
        toep = sb("toep", [P, NG, 3 * P])
        w1 = sb("w1", [P, E, F])
        w1f = sb("w1f", [P, F])
        w1h = sb("w1h", [P, E * F], f16)
        w1l = sb("w1l", [P, E * F], f16)
        w2 = sb("w2", [P, E * FB * D])
        b1s = sb("b1s", [P, E * FB])
        b2b = sb("b2b", [P, E * D])
        gS = sb("gS", [P, E])
        x = sb("x", [P, NT, D])
        xT = sb("xT", [P, NT, P])
        v = sb("v", [P, NT, D])
        xc = sb("xc", [P, NT, E])
        att = sb("att", [P, 4, NB, D])
        attT = sb("attT", [P, 4, NB, P])
        st1 = sb("st1", [P, NT, 6])
        mv1 = sb("mv1", [P, NT, 2])
        rs1 = sb("rs1", [P, NT])
        sq_junk = sb("sq_junk", [P, D])
        ssq = sb("ssq", [P, NT])
        rso = sb("rso", [P, NT])
        x1 = sb("x1", [P, NT, ROW])
        st2 = sb("st2", [P, NT, 6])
        ocr = sb("ocr", [P, NT, E])
        lg = sb("lg", [P, NT, E])
        colsum = sb("colsum", [P, 2])
        csum = sb("csum", [E, 1])
        mx = sb("mx", [P, NT])
        key = sb("key", [P, NT, E])
        hot = sb("hot", [P, 2 * NT + 1, E], bf16)
        cmpt = sb("cmpt", [P, E, NT])
        ntile = sb("ntile", [P, E])
        tend = sb("tend", [P, E])
        tstart = sb("tstart", [P, E])
        posf = sb("posf", [P, NT, E])
        pos = sb("pos", [P, NT], i32)
        pos_hi = sb("pos_hi", [P, NT], i32)
        pos_lo = sb("pos_lo", [P, NT], i32)
        lo_f = sb("lo_f", [P, NT])
        hi_hot = sb("hi_hot", [P, NT, CAP], bf16)
        lo_hot = sb("lo_hot", [P, NT, P], bf16)
        code = sb("code", [P, NT, 2, CAP], bf16)
        tok = sb("tok", [P, 2 * CAP])
        tokn = sb("tokn", [P, CAP])
        inv = sb("inv", [P, CAP])
        src_i = sb("src_i", [P, CAP], i32)
        dst_i = sb("dst_i", [P, CAP], i32)
        ecmp = sb("ecmp", [1, CAP, E])
        ef = sb("ef", [1, CAP])
        etab = sb("etab", [1, CAP], i32)
        xg = sb("xg", [P, CAP, ROW])
        xn = sb("xn", [P, 2, D])
        xb = sb("xb", [P, 2, D])
        xh = sb("xh", [P, 2, P], f16)
        xl = sb("xl", [P, 2, P], f16)
        h = sb("h", [P, 2, FB, P])
        z = sb("z", [P, 2, D])
        st3 = sb("st3", [P, 2, 6])
        mv3 = sb("mv3", [P, 2, 2])
        sd3 = sb("sd3", [P, 2])
        rs3 = sb("rs3", [P, 2])
        zn = sb("zn", [P, 2, D])
        o = sb("o", [P, CAP, D])

        l_small, l_wi, l_wo, l_toep = sem("l_small"), sem("l_wi"), sem("l_wo"), sem("l_toep")
        l_x = [sem(f"l_x{q}") for q in range(4)]
        l_w1 = [sem(f"l_w1{q}") for q in range(2)]
        l_w2, l_b2 = sem("l_w2"), sem("l_b2")
        c_pool, c_dve = sem("c_pool"), sem("c_dve")
        p_small, p_smallT, p_T, p_w, p_woc = sem("p_small"), sem("p_smallT"), sem("p_T"), sem("p_w"), sem("p_woc")
        p_gS, p_w1f, p_w1h, p_w1l, p_b1, p_b1s = (sem("p_gS"), sem("p_w1f"), sem("p_w1h"), sem("p_w1l"),
                                                  sem("p_b1"), sem("p_b1s"))
        a_st, a_var, a_sd, a_rs = sem("a_st"), sem("a_var"), sem("a_sd"), sem("a_rs")
        a_T, a_Te, a_v, a_ve, a_c, a_ce = (sem("a_T"), sem("a_Te"), sem("a_v"), sem("a_ve"), sem("a_c"), sem("a_ce"))
        a_o, a_sq, a_osd, a_ors, a_x1, a_oc, a_oe = (sem("a_o"), sem("a_sq"), sem("a_osd"), sem("a_ors"),
                                                     sem("a_x1"), sem("a_oc"), sem("a_oe"))
        a_st2, a_var2, a_sd2, a_row, a_lg = sem("a_st2"), sem("a_var2"), sem("a_sd2"), sem("a_row"), sem("a_lg")
        s_rows = sem("s_rows")
        r_dve, r_hot, r_rank, r_pos, r_lo, r_code, r_tok = (sem("r_dve"), sem("r_hot"), sem("r_rank"), sem("r_pos"),
                                                           sem("r_lo"), sem("r_code"), sem("r_tok"))
        r_idx, r_e = sem("r_idx"), sem("r_e")
        g_x = [sem(f"g_x{i}") for i in range(2)]
        s_out = sem("s_out")
        e_xn, e_xb, e_xT, e_xh, e_xl, e_h1a, e_h1b, e_ha, e_hb = (
            sem("e_xn"), sem("e_xb"), sem("e_xT"), sem("e_xh"), sem("e_xl"), sem("e_h1a"), sem("e_h1b"),
            sem("e_ha"), sem("e_hb"))
        e_y, e_z, e_st, e_var, e_sd, e_rs, e_zn, e_o = (sem("e_y"), sem("e_z"), sem("e_st"), sem("e_var"),
                                                       sem("e_sd"), sem("e_rs"), sem("e_zn"), sem("e_o"))

        bT = [bank[0], bank[1]]
        bV = [bank[2], bank[3]]
        bC = [bank[4], bank[5]]
        bO = [bank[6], bank[7]]

        def pair(b):
            return b[:, 0:2 * CE].rearrange("p (t c) -> p t c", c=CE)

        rank = bank[2][:, 0:(NT + 1) * E].rearrange("p (t e) -> p t e", e=E)
        tok_ps = bank[3][:, 0:2 * CAP]
        b1_ps = bank[4][:, 0:E * FB]
        psX = [bank[0], bank[1]]
        psHa = [bank[2], bank[3]]
        psHb = [bank[4], bank[5]]
        psY = [bank[6], bank[7]]

        def otiles(n):
            hf, qb, bp = n // 4, (n // 2) % 2, n % 2
            t0 = HALF * hf + qb + 4 * bp
            return t0, t0 + 2

        LOOPS = (CAP - 5) // 2
        assert CAP - 5 == 2 * LOOPS

        block = ctx.enter_context(nc.Block())

        @block.sync
        def _(sp):
            sp.dma_start(small[0:E, :], cent_d).then_inc(l_small, 16)
            sp.dma_start(small[E:2 * E, :], lng_d).then_inc(l_small, 16)
            sp.dma_start(small[2 * E:3 * E, :], lnb_d).then_inc(l_small, 16)
            sp.dma_start(small[3 * E:NR, :], b1_d.rearrange("e (f p) -> (e f) p", p=P)).then_inc(l_small, 16)
            for q in range(4):
                sp.dma_start(x[:, 4 * q:4 * q + 4, :], x_view[:, 4 * q:4 * q + 4, :]).then_inc(l_x[q], 16)
            for q in range(2):
                sp.dma_start(w1[:, 4 * q:4 * q + 4, :], w1_d[4 * q:4 * q + 4].rearrange("e d f -> d e f"))\
                    .then_inc(l_w1[q], 16)
            sp.dma_start(w2[:, :].rearrange("p (e f d) -> p e f d", e=E, f=FB),
                         w2_d.rearrange("e (f p) d -> p e f d", p=P)).then_inc(l_w2, 16)
            for g in range(4):
                t0 = HALF * (g // 2) + g % 2
                sp.wait_ge(a_row, g + 1)
                sp.dma_start(x1_view[:, t0:t0 + 7:2, :], x1[:, t0:t0 + 7:2, :]).then_inc(s_rows, 16)

        @block.gpsimd
        def _(pool):
            g = nc.gpsimd
            g.memset(ident[:, :], 0.0).then_inc(c_pool, 1)
            g.memset(before[:, :], 1.0).then_inc(c_pool, 1)
            pool.wait_ge(c_pool, 2)
            g.affine_select(out=ident[:, :], in_=ident[:, :], compare_op=ALU.not_equal, fill=1.0, base=0,
                            pattern=[[-1, P]], channel_multiplier=1).then_inc(c_pool, 1)
            g.affine_select(out=before[:, :], in_=before[:, :], compare_op=ALU.is_gt, fill=0.0, base=0,
                            pattern=[[1, P]], channel_multiplier=-1).then_inc(c_pool, 1)
            g.iota(lane[:, :], pattern=[[1, P]], base=0, channel_multiplier=0,
                   allow_small_or_imprecise_dtypes=True).then_inc(c_pool, 1)
            g.iota(tile_no[:, :], pattern=[[1, CAP + 1]], base=0, channel_multiplier=0,
                   allow_small_or_imprecise_dtypes=True).then_inc(c_pool, 1)
            g.iota(tile_thr[:, :], pattern=[[P, NT]], base=0, channel_multiplier=0,
                   allow_small_or_imprecise_dtypes=True).then_inc(c_pool, 1)
            g.iota(first_wt[:, :], pattern=[[-1, E]], base=E, channel_multiplier=0,
                   allow_small_or_imprecise_dtypes=True).then_inc(c_pool, 1)
            g.iota(lane_col[:, :], pattern=[[0, 1]], base=1, channel_multiplier=1,
                   allow_small_or_imprecise_dtypes=True).then_inc(c_pool, 1)
            for e in range(E):
                if e == 0:
                    pool.wait_ge(p_gS, 1)
                if e % 4 == 0:
                    pool.wait_ge(l_w1[e // 4], 16)
                if e:
                    pool.wait_ge(p_w1l, e)
                cols = slice(e * F, (e + 1) * F)
                g.tensor_scalar(w1f[:, :], w1[:, e, :], gS[:, e:e + 1], None, ALU.mult).then_inc(p_w1f, 1)
                pool.wait_ge(p_w1f, e + 1)
                g.tensor_copy(w1h[:, cols], w1f[:, :]).then_inc(p_w1h, 1)
                pool.wait_ge(p_w1h, e + 1)
                g.tensor_tensor(w1l[:, cols], w1f[:, :], w1h[:, cols], ALU.subtract).then_inc(p_w1l, 1)

            def gather(j):
                if j >= 2:
                    pool.wait_ge(g_x[j % 2], 16 * (j // 2))
                g.indirect_dma_start(out=xg[:, j, :], out_offset=None, in_=x1_dram,
                                     in_offset=bass.IndirectOffsetOnAxis(ap=src_i[:, j:j + 1].bitcast(u32), axis=0))\
                    .then_inc(g_x[j % 2], 16)

            def scatter(j):
                pool.wait_ge(e_o, j + 1)
                g.indirect_dma_start(out=out_rows,
                                     out_offset=bass.IndirectOffsetOnAxis(ap=dst_i[:, j:j + 1].bitcast(u32), axis=0),
                                     in_=o[:, j, :], in_offset=None, bounds_check=T - 1, oob_is_err=False)\
                    .then_inc(s_out, 16)

            pool.wait_ge(r_idx, 2)
            pool.wait_ge(s_rows, 64)
            for j in range(4):
                gather(j)
            pool.wait_ge(r_e, 1)
            pool.wait_ge(l_b2, 16)
            for j in range(CAP):
                if j + 4 < CAP:
                    gather(j + 4)
                e_j = pool.value_load(etab[0:1, j:j + 1], min_val=0, max_val=E - 1)
                pool.wait_ge(e_xn, j + 1)
                if j >= 2:
                    pool.wait_ge(e_z, j - 1)
                g.tensor_tensor(xb[:, j % 2, :], xn[:, j % 2, :], b2b[:, bass.ds(e_j * D, D)], ALU.add)\
                    .then_inc(e_xb, 1)
                if j:
                    scatter(j - 1)
            scatter(CAP - 1)
            pool.wait_ge(s_out, 16 * CAP)

        @block.scalar
        def _(act):
            s = nc.scalar
            act.dma_start(wi[:, :], wi_d).then_inc(l_wi, 16)
            act.dma_start(wo[:, :], wo_d).then_inc(l_wo, 16)
            act.dma_start(toep[:, :, :], toep_d.rearrange("p (g c) -> p g c", g=NG)).then_inc(l_toep, 16)
            act.dma_start(b2b[:, :], b2_d.rearrange("e d -> (e d)").partition_broadcast(P)).then_inc(l_b2, 16)
            act.wait_ge(c_dve, 1)

            def evac_T(n):
                dst = xT[:, 4 * n:4 * n + 4, :] if n < 4 else attT[:, n - 4, :, :]
                act.wait_ge(a_T, n + 1)
                s.activation(dst, bT[n % 2][:, :].rearrange("p (t c) -> p t c", c=P), ACT.Copy).then_inc(a_Te, 1)

            def sd_1(q):
                act.wait_ge(a_var, 4 * q + 4)
                s.activation(rs1[:, 4 * q:4 * q + 4], mv1[:, 4 * q:4 * q + 4, 1], ACT.Sqrt, bias=eps_t[:, 0:1])\
                    .then_inc(a_sd, 1)

            def evac_C(c):
                act.wait_ge(a_c, c + 1)
                s.activation(att[:, c, :, :], bC[c % 2][:, :].rearrange("p (b d) -> p b d", d=D), ACT.Copy)\
                    .then_inc(a_ce, 1)

            def o_stats(n):
                act.wait_ge(a_o, n + 1)
                for k, t in enumerate(otiles(n)):
                    if 2 * n + k:
                        act.wait_ge(a_sq, 2 * n + k)
                    s.activation(sq_junk[:, :], pair(bO[n % 2])[:, k, 0:D], ACT.Square, accum_out=ssq[:, t:t + 1])\
                        .then_inc(a_sq, 1)
                t0, t1 = otiles(n)
                act.wait_ge(a_sq, 2 * n + 2)
                s.activation(rso[:, t0:t1 + 1:2], ssq[:, t0:t1 + 1:2], ACT.Sqrt, bias=eps_t[:, 0:1], scale=1.0 / D)\
                    .then_inc(a_osd, 1)

            def sd_2(gr):
                t0 = HALF * (gr // 2) + gr % 2
                act.wait_ge(a_var2, 4 * gr + 4)
                s.activation(x1[:, t0:t0 + 7:2, D + 1], x1[:, t0:t0 + 7:2, D + 1], ACT.Sqrt, bias=eps_t[:, 0:1])\
                    .then_inc(a_sd2, 1)

            for q in (0, 1):
                evac_T(q)
                sd_1(q)
            for q in (2, 3):
                evac_T(q)
                sd_1(q)
            evac_C(0)
            evac_C(1)
            evac_T(4)
            evac_T(5)
            evac_C(2)
            evac_C(3)
            for n in range(4):
                o_stats(n)
                if n == 1:
                    evac_T(6)
                    evac_T(7)
                if n == 2:
                    sd_2(0)
            for n in range(4, 8):
                o_stats(n)
                if n == 4:
                    sd_2(1)
                if n == 6:
                    sd_2(2)
            sd_2(3)

            def expert_of(i, c):
                return act.value_load(etab[0:1, bass.ds(2 * i + c, 1)], min_val=0, max_val=E - 1)

            def high(i, c):
                j = 2 * i + c
                act.wait_ge(e_xT, j + 1)
                if c >= 1:
                    act.wait_ge(e_h1b, j - 1)
                s.activation(xh[:, c % 2, :], psX[c % 2][:, 0:P], ACT.Copy).then_inc(e_xh, 1)

            def hidden_a(i, c):
                j = 2 * i + c
                e_j = expert_of(i, c)
                act.wait_ge(e_h1a, j + 1)
                if c >= 1:
                    act.wait_ge(e_y, j - 1)
                s.activation(h[:, c % 2, 0, :], psHa[c % 2][:, 0:P], ACT.Relu, bias=b1s[:, bass.ds(e_j * FB, 1)])
                s.activation(h[:, c % 2, 1, :], psHa[c % 2][:, P:2 * P], ACT.Relu,
                             bias=b1s[:, bass.ds(e_j * FB + 1, 1)]).then_inc(e_ha, 1)

            def sd_3(i, c):
                act.wait_ge(e_var, 2 * i + c + 1)
                s.activation(sd3[:, c % 2:c % 2 + 1], mv3[:, c % 2, 1:2], ACT.Sqrt, bias=eps_t[:, 0:1])\
                    .then_inc(e_sd, 1)

            act.wait_ge(r_e, 1)
            act.wait_ge(p_b1s, 1)
            def slot(i, c, more=True):
                if more:
                    high(i, c + 1)
                hidden_a(i, c)
                if c >= 1:
                    sd_3(i, c - 1)

            high(0, 0)
            slot(0, 0)
            slot(0, 1)
            with act.Fori(0, LOOPS) as i:
                slot(i, 2)
                slot(i, 3)
            slot(LOOPS, 2)
            slot(LOOPS, 3)
            slot(LOOPS, 4, more=False)
            sd_3(LOOPS, 4)

        @block.vector
        def _(dve):
            d = nc.vector
            d.memset(eps_t[:, :], EPS).then_inc(c_dve, 1)
            d.memset(ones_bf[:, :], 1.0).then_inc(c_dve, 1)
            d.memset(ones_e[:, :], 1.0).then_inc(c_dve, 1)
            d.memset(hot[:, :, :], 0.0).then_inc(c_dve, 1)

            def x_stats(q):
                dve.wait_ge(l_x[q], 16)
                for t in range(4 * q, 4 * q + 4):
                    d.bn_stats(st1[:, t, :], x[:, t, :]).then_inc(a_st, 1)
                for t in range(4 * q, 4 * q + 4):
                    dve.wait_ge(a_st, t + 1)
                    d.bn_aggr(mv1[:, t, :], st1[:, t, :]).then_inc(a_var, 1)

            def x_rstd(q):
                dve.wait_ge(a_sd, q + 1)
                d.reciprocal(rs1[:, 4 * q:4 * q + 4], rs1[:, 4 * q:4 * q + 4]).then_inc(a_rs, 1)

            dve.wait_ge(l_small, 64)
            d.reduce_sum(csum[:, :], small[0:E, :], AX.X).then_inc(p_small, 1)
            dve.wait_ge(p_small, 1)
            d.tensor_scalar(csum[:, :], csum[:, :], -1.0 / D, None, ALU.mult).then_inc(p_small, 1)
            dve.wait_ge(p_small, 2)
            d.tensor_scalar(small[0:E, :], small[0:E, :], csum[:, 0:1], None, ALU.add).then_inc(p_small, 1)
            dve.wait_ge(l_wi, 16)
            d.reduce_sum(colsum[:, 0:1], wi[:, :], AX.X).then_inc(p_small, 1)
            dve.wait_ge(p_small, 4)
            d.tensor_scalar(colsum[:, 0:1], colsum[:, 0:1], -1.0 / D, None, ALU.mult).then_inc(p_small, 1)
            dve.wait_ge(p_small, 5)
            d.tensor_scalar(wi[:, :], wi[:, :], colsum[:, 0:1], None, ALU.add).then_inc(p_small, 1)
            dve.wait_ge(p_T, 1)
            d.tensor_copy(smallT[:, :], bank[7][:, 0:NR]).then_inc(p_smallT, 1)
            dve.wait_ge(p_smallT, 1)
            d.tensor_scalar(gS[:, :], smallT[:, E:2 * E], S, None, ALU.mult).then_inc(p_gS, 1)
            d.tensor_copy(wxc[:, D:CE], smallT[:, 0:E]).then_inc(p_w, 1)
            dve.wait_ge(p_T, 2)
            d.tensor_copy(wxc[:, 0:D], bank[6][:, 0:P]).then_inc(p_w, 1)
            dve.wait_ge(p_T, 3)
            d.reduce_sum(colsum[:, 1:2], bank[5][:, 0:P], AX.X).then_inc(p_w, 1)
            dve.wait_ge(p_w, 3)
            d.tensor_scalar(colsum[:, 1:2], colsum[:, 1:2], -1.0 / D, None, ALU.mult).then_inc(p_w, 1)
            dve.wait_ge(p_w, 4)
            d.tensor_scalar(woc[:, 0:D], bank[5][:, 0:P], colsum[:, 1:2], None, ALU.add).then_inc(p_w, 1)
            dve.wait_ge(p_woc, 1)
            d.tensor_copy(woc[:, D:CE], bank[4][:, 0:E]).then_inc(p_w, 1)

            def values(n):
                dve.wait_ge(a_v, n + 1)
                t0 = 2 * n
                if n % 2 == 0:
                    dve.wait_ge(a_rs, n // 2 + 1)
                src = pair(bV[n % 2])
                d.tensor_tensor(v[:, t0:t0 + 2, :], src[:, :, 0:D],
                                rs1[:, t0:t0 + 2].unsqueeze(2).broadcast_to([P, 2, D]), ALU.mult)
                d.tensor_copy(xc[:, t0:t0 + 2, :], src[:, :, D:CE]).then_inc(a_ve, 1)

            def residual(n):
                t0, t1 = otiles(n)
                two = slice(t0, t1 + 1, 2)
                dve.wait_ge(a_osd, n + 1)
                d.reciprocal(rso[:, two], rso[:, two]).then_inc(a_ors, 1)
                dve.wait_ge(a_ors, n + 1)
                src = pair(bO[n % 2])
                for k, t in enumerate((t0, t1)):
                    d.scalar_tensor_tensor(x1[:, t, 0:D], src[:, k, 0:D], rso[:, t:t + 1], x[:, t, :],
                                           ALU.mult, ALU.add).then_inc(a_x1, 1)
                d.tensor_tensor(ocr[:, two, :], src[:, :, D:CE], rso[:, two].unsqueeze(2).broadcast_to([P, 2, E]),
                                ALU.mult).then_inc(a_oe, 1)
                dve.wait_ge(a_oe, n + 1)
                d.tensor_tensor(lg[:, two, :], ocr[:, two, :], xc[:, two, :], ALU.add).then_inc(a_lg, 1)
                for k, t in enumerate((t0, t1)):
                    dve.wait_ge(a_x1, 2 * n + k + 1)
                    d.bn_stats(st2[:, t, :], x1[:, t, 0:D]).then_inc(a_st2, 1)
                for k, t in enumerate((t0, t1)):
                    dve.wait_ge(a_st2, 2 * n + k + 1)
                    d.bn_aggr(x1[:, t, D:ROW], st2[:, t, :]).then_inc(a_var2, 1)

            def row_rstd(gr):
                t0 = HALF * (gr // 2) + gr % 2
                dve.wait_ge(a_sd2, gr + 1)
                d.reciprocal(x1[:, t0:t0 + 7:2, D + 1], x1[:, t0:t0 + 7:2, D + 1]).then_inc(a_row, 1)

            for q in (0, 1):
                x_stats(q)
            for q in (0, 1):
                x_rstd(q)
            for n in range(4):
                values(n)
            for q in (2, 3):
                x_stats(q)
            for q in (2, 3):
                x_rstd(q)
            for n in range(4, 8):
                values(n)
            for n in range(8):
                residual(n)
                if n in (3, 5, 7):
                    row_rstd((n - 3) // 2)
            row_rstd(3)

            step = [0]

            def link(ins):
                step[0] += 1
                ins.then_inc(r_dve, 1)
                dve.wait_ge(r_dve, step[0])

            def over_e(a):
                return a.unsqueeze(2).broadcast_to([P, NT, E])

            dve.wait_ge(a_lg, 8)
            dve.wait_ge(c_pool, 9)
            hot_t = hot[:, NT:2 * NT, :]
            link(d.reduce_max(mx[:, :], lg[:, :, :], AX.X))
            link(d.tensor_tensor(key[:, :, :], lg[:, :, :], over_e(mx[:, :]), ALU.is_equal))
            link(d.tensor_tensor(key[:, :, :], key[:, :, :], first_wt[:, :].unsqueeze(1).broadcast_to([P, NT, E]),
                                 ALU.mult))
            link(d.reduce_max(mx[:, :], key[:, :, :], AX.X))
            dve.wait_ge(c_dve, 4)
            d.tensor_tensor(hot_t, key[:, :, :], over_e(mx[:, :]), ALU.is_equal).then_inc(r_hot, 1)
            dve.wait_ge(r_rank, 1)
            link(d.tensor_tensor(cmpt[:, :, :], rank[:, NT, :].unsqueeze(2).broadcast_to([P, E, NT]),
                                 tile_thr[:, :].unsqueeze(1).broadcast_to([P, E, NT]), ALU.is_gt))
            link(d.reduce_sum(ntile[:, :], cmpt[:, :, :], AX.X))
            link(d.tensor_tensor_scan(tend[:, :], ones_e[:, :], ntile[:, :], 0.0, ALU.mult, ALU.add))
            link(d.tensor_tensor(tstart[:, :], tend[:, :], ntile[:, :], ALU.subtract))
            link(d.scalar_tensor_tensor(posf[:, :, :], tstart[:, :].unsqueeze(1).broadcast_to([P, NT, E]), float(P),
                                        rank[:, 0:NT, :], ALU.mult, ALU.add))
            link(d.tensor_tensor(posf[:, :, :], posf[:, :, :], hot_t, ALU.mult))
            link(d.reduce_sum(mx[:, :], posf[:, :, :], AX.X))
            link(d.tensor_copy(pos[:, :], mx[:, :]))
            link(d.tensor_scalar(pos_lo[:, :], pos[:, :], P - 1, None, ALU.bitwise_and))
            link(d.tensor_copy(lo_f[:, :], pos_lo[:, :]))
            for t in range(NT):
                d.tensor_scalar(lo_hot[:, t, :], lane[:, :], lo_f[:, t:t + 1], None, ALU.is_equal)\
                    .then_inc(r_lo, 1)
            link(d.tensor_scalar(pos_hi[:, :], pos[:, :], 7, None, ALU.arith_shift_right))
            link(d.tensor_tensor(hi_hot[:, :, :], pos_hi[:, :].unsqueeze(2).broadcast_to([P, NT, CAP]),
                                 tile_no[:, 0:CAP].unsqueeze(1).broadcast_to([P, NT, CAP]), ALU.is_equal))
            d.tensor_scalar(code[:, :, 0, :], hi_hot[:, :, :], lane_col[:, 0:1], None, ALU.mult).then_inc(r_code, 1)
            d.tensor_tensor(code[:, :, 1, :], hi_hot[:, :, :],
                            tile_no[:, 0:NT].unsqueeze(2).broadcast_to([P, NT, CAP]), ALU.mult).then_inc(r_code, 1)
            link(d.tensor_tensor(ecmp[:, :, :], tend[0:1, :].unsqueeze(1).broadcast_to([1, CAP, E]),
                                 tile_no[0:1, 0:CAP].unsqueeze(2).broadcast_to([1, CAP, E]), ALU.is_le))
            link(d.reduce_sum(ef[:, :], ecmp[:, :, :], AX.X))
            d.tensor_scalar(etab[:, :], ef[:, :], float(E - 1), None, ALU.min).then_inc(r_e, 1)
            dve.wait_ge(p_b1, 1)
            link(d.tensor_tensor(b1s[:, :], b1_ps, smallT[:, 3 * E:NR], ALU.add))
            d.tensor_scalar(b1s[:, :], b1s[:, :], S, None, ALU.mult).then_inc(p_b1s, 1)
            dve.wait_ge(r_tok, 1)
            link(d.tensor_copy(tok[:, :], tok_ps))
            link(d.scalar_tensor_tensor(tokn[:, :], tok[:, CAP:2 * CAP], float(P), tok[:, 0:CAP], ALU.mult, ALU.add))
            d.tensor_scalar(src_i[:, :], tokn[:, :], -1.0, 0.0, ALU.add, ALU.max).then_inc(r_idx, 1)
            link(d.tensor_scalar(inv[:, :], tokn[:, :], 0.5, 2.0 * T, ALU.is_lt, ALU.mult))
            d.scalar_tensor_tensor(dst_i[:, :], tokn[:, :], -1.0, inv[:, :], ALU.add, ALU.add).then_inc(r_idx, 1)

            def norm(i, c):
                j = 2 * i + c
                dve.wait_ge(g_x[c % 2], 16 * (i + c // 2 + 1))
                if c >= 1:
                    dve.wait_ge(e_xT, j - 1)
                    dve.wait_ge(e_xb, j - 1)
                row = xg[:, bass.ds(j, 1), :].rearrange("p a c -> p (a c)")
                d.tensor_scalar(xn[:, c % 2, :], row[:, 0:D], row[:, D:D + 1], row[:, D + 1:ROW],
                                ALU.subtract, ALU.mult).then_inc(e_xn, 1)

            def low(i, c):
                dve.wait_ge(e_xh, 2 * i + c + 1)
                d.tensor_tensor(xl[:, c % 2, :], psX[c % 2][:, 0:P], xh[:, c % 2, :], ALU.subtract)\
                    .then_inc(e_xl, 1)

            def hidden_b(i, c):
                j = 2 * i + c
                if c == 0:
                    dve.wait_ge(r_e, 1)
                    dve.wait_ge(p_b1s, 1)
                e_j = dve.value_load(etab[0:1, bass.ds(j, 1)], min_val=0, max_val=E - 1)
                dve.wait_ge(e_h1b, j + 1)
                if c >= 1:
                    dve.wait_ge(e_y, j - 1)
                d.tensor_scalar(h[:, c % 2, 2, :], psHb[c % 2][:, 0:P], b1s[:, bass.ds(e_j * FB + 2, 1)], 0.0,
                                ALU.add, ALU.max)
                d.tensor_scalar(h[:, c % 2, 3, :], psHb[c % 2][:, P:2 * P], b1s[:, bass.ds(e_j * FB + 3, 1)], 0.0,
                                ALU.add, ALU.max).then_inc(e_hb, 1)

            def output_stats(i, c):
                j = 2 * i + c
                dve.wait_ge(e_y, j + 1)
                dve.wait_ge(e_xb, j + 1)
                d.scalar_tensor_tensor(z[:, c % 2, :], psY[c % 2][:, 0:D], 1.0 / S, xb[:, c % 2, :],
                                       ALU.mult, ALU.add).then_inc(e_z, 1)
                dve.wait_ge(e_z, j + 1)
                d.bn_stats(st3[:, c % 2, :], z[:, c % 2, :]).then_inc(e_st, 1)

            def output_var(i, c):
                d.bn_aggr(mv3[:, c % 2, :], st3[:, c % 2, :]).then_inc(e_var, 1)

            def output(i, c):
                j = 2 * i + c
                dve.wait_ge(e_sd, j + 1)
                d.reciprocal(rs3[:, c % 2:c % 2 + 1], sd3[:, c % 2:c % 2 + 1]).then_inc(e_rs, 1)
                dve.wait_ge(e_rs, j + 1)
                d.tensor_scalar(zn[:, c % 2, :], z[:, c % 2, :], mv3[:, c % 2, 0:1], rs3[:, c % 2:c % 2 + 1],
                                ALU.subtract, ALU.mult).then_inc(e_zn, 1)
                dve.wait_ge(e_zn, j + 1)
                d.tensor_tensor(o[:, bass.ds(j, 1), :], zn[:, c % 2:c % 2 + 1, :], xg[:, bass.ds(j, 1), 0:D],
                                ALU.add).then_inc(e_o, 1)

            def slot(i, c, ahead=2):
                if ahead >= 1:
                    low(i, c + 1)
                hidden_b(i, c)
                if c >= 1:
                    output_stats(i, c - 1)
                    dve.wait_ge(e_st, 2 * i + c)
                if ahead >= 2:
                    norm(i, c + 2)
                if c >= 1:
                    output_var(i, c - 1)
                    output(i, c - 1)

            norm(0, 0)
            norm(0, 1)
            low(0, 0)
            slot(0, 0)
            slot(0, 1)
            with dve.Fori(0, LOOPS) as i:
                slot(i, 2)
                slot(i, 3)
            slot(LOOPS, 2)
            slot(LOOPS, 3, ahead=1)
            slot(LOOPS, 4, ahead=0)
            output_stats(LOOPS, 4)
            dve.wait_ge(e_st, CAP)
            output_var(LOOPS, 4)
            output(LOOPS, 4)

        @block.tensor
        def _(pe):
            t_ = nc.tensor

            def transposes(n, src, done):
                if n >= 2:
                    pe.wait_ge(a_Te, n - 1)
                for k in range(4):
                    last = t_.transpose(bT[n % 2][:, k * P:(k + 1) * P], src[k], ident[:, :])
                last.then_inc(done, 1)

            def x_T(q):
                pe.wait_ge(l_x[q], 16)
                transposes(q, [x[:, 4 * q + k, :] for k in range(4)], a_T)

            def att_T(n):
                pe.wait_ge(a_ce, n - 3)
                transposes(n, [att[:, n - 4, k, :] for k in range(4)], a_T)

            def project_x(n):
                if n % 2 == 0:
                    pe.wait_ge(a_Te, n // 2 + 1)
                if n >= 2:
                    pe.wait_ge(a_ve, n - 1)
                for k in range(2):
                    last = t_.matmul(pair(bV[n % 2])[:, k, :], xT[:, 2 * n + k, :], wxc[:, :], start=True, stop=True)
                last.then_inc(a_v, 1)

            def attend(c):
                hf, qb = c // 2, c % 2
                if c >= 1:
                    pe.wait_ge(a_ce, c - 1)
                dst = bC[c % 2][:, :].rearrange("p (b u g i) -> p b u g i", b=NB, u=2, g=NG)
                val = v[:, HALF * hf:HALF * (hf + 1), :].rearrange("p (b k) (u g i) -> p k b u g i", k=2, u=2, g=NG)
                for g in range(NG):
                    for kb in range(2):
                        off = P * (1 - kb + qb)
                        last = t_.matmul(dst[:, :, :, g, :], toep[:, g, off:off + P], val[:, kb, :, :, g, :],
                                         start=(kb == 0), stop=(kb == 1))
                last.then_inc(a_c, 1)

            def project_o(n):
                if n % 2 == 0:
                    pe.wait_ge(a_Te, n // 2 + 5)
                if n >= 2:
                    pe.wait_ge(a_lg, n - 1)
                for k in range(2):
                    last = t_.matmul(pair(bO[n % 2])[:, k, :], attT[:, n // 2, 2 * (n % 2) + k, :], woc[:, :],
                                     start=True, stop=True)
                last.then_inc(a_o, 1)

            pe.wait_ge(c_pool, 3)
            x_T(0)
            x_T(1)
            pe.wait_ge(p_small, 3)
            t_.transpose(bank[7][:, 0:NR], small[:, :], ident[0:NR, 0:NR]).then_inc(p_T, 1)
            pe.wait_ge(p_small, 6)
            t_.transpose(bank[6][:, 0:P], wi[:, :], ident[:, :]).then_inc(p_T, 1)
            pe.wait_ge(l_wo, 16)
            t_.transpose(bank[5][:, 0:P], wo[:, :], ident[:, :]).then_inc(p_T, 1)
            pe.wait_ge(p_smallT, 1)
            t_.matmul(bank[4][:, 0:E], wo[:, :], smallT[:, 0:E], start=True, stop=True).then_inc(p_woc, 1)
            pe.wait_ge(p_w, 6)
            for n in range(4):
                project_x(n)
            x_T(2)
            x_T(3)
            pe.wait_ge(l_toep, 16)
            pe.wait_ge(a_ve, 4)
            attend(0)
            attend(1)
            for n in range(4, 8):
                project_x(n)
            att_T(4)
            att_T(5)
            pe.wait_ge(a_ve, 8)
            attend(2)
            attend(3)
            for n in range(4):
                project_o(n)
            att_T(6)
            att_T(7)
            for n in range(4, 8):
                project_o(n)
            for q in range(2):
                pe.wait_ge(l_w1[q], 16)
            pe.wait_ge(a_ce, 4)
            for e in range(E):
                for f in range(FB):
                    last = t_.matmul(b1_ps[:, e * FB + f:e * FB + f + 1], w1[:, e, f * P:(f + 1) * P],
                                     smallT[:, 2 * E + e:2 * E + e + 1], start=True, stop=True)
            last.then_inc(p_b1, 1)

            pe.wait_ge(c_pool, 4)
            pe.wait_ge(c_dve, 4)
            pe.wait_ge(r_hot, 1)
            for k in range(NT, 0, -1):
                t_.matmul(rank[:, :, :], ones_bf[:, :], hot[:, NT - k:2 * NT + 1 - k, :], start=(k == NT), stop=False)
            t_.matmul(rank[:, :, :], before[:, :], hot[:, NT:2 * NT + 1, :], start=False, stop=True)\
                .then_inc(r_rank, 1)
            pe.wait_ge(r_code, 2)
            for t in range(NT):
                pe.wait_ge(r_lo, t + 1)
                last = t_.matmul(tok_ps, lo_hot[:, t, :], code[:, t, :, :], start=(t == 0), stop=(t == NT - 1))
            last.then_inc(r_tok, 1)

            def expert_of(i, c):
                return pe.value_load(etab[0:1, bass.ds(2 * i + c, 1)], min_val=0, max_val=E - 1)

            def input_T(i, c):
                j = 2 * i + c
                pe.wait_ge(e_xn, j + 1)
                if c >= 1:
                    pe.wait_ge(e_xl, j - 1)
                t_.transpose(psX[c % 2][:, 0:P], xn[:, c % 2, :], ident[:, :]).then_inc(e_xT, 1)

            def up(i, c):
                j = 2 * i + c
                e_j = expert_of(i, c)
                pe.wait_ge(e_xl, j + 1)
                if c >= 1:
                    pe.wait_ge(e_ha, j - 1)
                    pe.wait_ge(e_hb, j - 1)
                for f in range(FB):
                    dst = (psHa, psHb)[f // 2][c % 2][:, (f % 2) * P:(f % 2 + 1) * P]
                    cols = bass.ds(e_j * F + f * P, P)
                    t_.matmul(dst, w1h[:, cols], xh[:, c % 2, :], start=True, stop=False)
                    t_.matmul(dst, w1h[:, cols], xl[:, c % 2, :], start=False, stop=False)
                    last = t_.matmul(dst, w1l[:, cols], xh[:, c % 2, :], start=False, stop=True)
                    if f % 2:
                        last.then_inc((e_h1a, e_h1b)[f // 2], 1)

            def down(i, c):
                j = 2 * i + c
                e_j = expert_of(i, c)
                pe.wait_ge(e_ha, j + 1)
                pe.wait_ge(e_hb, j + 1)
                if c >= 1:
                    pe.wait_ge(e_z, j - 1)
                for f in range(FB):
                    last = t_.matmul(psY[c % 2][:, 0:D], h[:, c % 2, f, :],
                                     w2[:, bass.ds(e_j * (FB * D) + f * D, D)], start=(f == 0), stop=(f == FB - 1))
                last.then_inc(e_y, 1)

            pe.wait_ge(r_e, 1)
            pe.wait_ge(p_w1l, E)
            pe.wait_ge(l_w2, 16)
            def slot(i, c, more=True):
                if more:
                    input_T(i, c + 1)
                up(i, c)
                if c >= 1:
                    down(i, c - 1)

            input_T(0, 0)
            slot(0, 0)
            slot(0, 1)
            with pe.Fori(0, LOOPS) as i:
                slot(i, 2)
                slot(i, 3)
            slot(LOOPS, 2)
            slot(LOOPS, 3)
            slot(LOOPS, 4, more=False)
            down(LOOPS, 4)


_INS = ['L0_attn_values', 'L0_attn_input_weights', 'L0_attn_output_weight', 'L0_ffn_centroids', 'L0_ffn_ln_g',
        'L0_ffn_ln_b', 'L0_ffn_W1', 'L0_ffn_b1', 'L0_ffn_W2', 'L0_ffn_b2']


def toeplitz_table(np):
    dist = (np.arange(128)[:, None] - np.arange(384)[None, :] + 128).astype(np.float32)
    parts = []
    for std, off in zip(ATTN_STD, ATTN_OFFSET):
        std, off = np.float32(std), np.float32(off)
        norm = np.float32(1.0 / (float(std) * np.sqrt(2.0 * np.pi)))
        parts.append(norm * np.exp(np.float32(-0.5) * ((dist - off) / std) ** 2))
    return np.stack(parts, 1).reshape(128, -1).astype(np.float32)


def kernel(**inputs):
    import numpy as _np
    import concourse.bacc as _bacc
    from concourse import mybir as _mybir
    from concourse.bass_utils import run_bass_kernel_spmd as _run

    nc = _bacc.Bacc("TRN2", target_bir_lowering=False, num_devices=1)
    arrays, args = {}, []
    for name in _INS:
        a = _np.ascontiguousarray(inputs[name])
        arrays[f"in_{name}_dram"] = a
        args.append(nc.dram_tensor(f"in_{name}_dram", a.shape, _mybir.dt.from_np(a.dtype), kind="ExternalInput").ap())
    table = toeplitz_table(_np)
    arrays["in_toeplitz_dram"] = table
    args.append(nc.dram_tensor("in_toeplitz_dram", table.shape, _mybir.dt.float32, kind="ExternalInput").ap())
    shape = inputs['L0_attn_values'].shape
    args.append(nc.dram_tensor("out_0_dram", shape, _mybir.dt.float32, kind="ExternalOutput").ap())
    attention_moe_block(nc, *args)
    r = _run(nc, [arrays], core_ids=[0])
    return r.results[0]["out_0_dram"]
```

```python
import concourse.bass as bass
from concourse import mybir
from contextlib import ExitStack

ATTN_STD = (1.0, 2.0, 4.0, 8.0)
ATTN_OFFSET = (-1.0, -2.0, -4.0, -8.0)


def attention_moe_block(nc, x_d, wi_d, wo_d, cent_d, lng_d, lnb_d, w1_d, b1_d, w2_d, b2_d, toep_d, out_d):
    fp32, bf16, f16, i32 = mybir.dt.float32, mybir.dt.bfloat16, mybir.dt.float16, mybir.dt.int32
    u32 = mybir.dt.uint32
    ALU, ACT, AX = mybir.AluOpType, mybir.ActivationFunctionType, mybir.AxisListType

    P = 128
    B, L, D = x_d.shape
    E, _, F = w1_d.shape
    T = B * L
    NT = T // P
    FB = F // P
    CAP = NT + E - 1
    NG = len(ATTN_STD)
    HD = D // (2 * NG)
    HALF = NT // 2
    NB = HALF // 2
    EPS = 1e-5
    S = 64.0
    ROW = D + 4
    CE = D + E
    NR = 2 * E + FB * E

    REGION = T + P
    SPARE = CAP - NT
    NOWHERE = 2 * T
    GT = 4
    rows_dram = nc.dram_tensor("expert_rows", [E * REGION + SPARE * P, ROW], fp32, kind="Internal").ap()
    b2_dram = nc.dram_tensor("b2_parts", [3, E, D], bf16, kind="Internal").ap()
    x_view = x_d.rearrange("b l d -> (b l) d").rearrange("(t p) d -> p t d", p=P)
    out_rows = out_d.rearrange("b l d -> (b l) d")

    ctx = ExitStack()
    with ctx:
        def sb(name, shape, dt=fp32):
            return ctx.enter_context(nc.sbuf_tensor(name, shape, dt))

        def sem(name):
            return ctx.enter_context(nc.semaphore(name))

        bank = [ctx.enter_context(nc.psum_tensor(f"bank{i}", [P, 512], fp32)) for i in range(8)]

        ident = sb("ident", [P, P])
        ones_bf = sb("ones_bf", [P, P], bf16)
        before = sb("before", [P, P], bf16)
        tile_no = sb("tile_no", [1, CAP])
        tile_thr = sb("tile_thr", [P, NT])
        first_wt = sb("first_wt", [P, E])
        region0 = sb("region0", [P, E])
        pad = sb("pad", [P, SPARE, ROW])
        ones_e = sb("ones_e", [P, E])
        eps_t = sb("eps_t", [P, 4])
        cent = sb("cent", [E, D])
        small = sb("small", [NR, D])
        smallT = sb("smallT", [P, NR])
        centring = sb("centring", [P, CE])
        wi = sb("wi", [P, D])
        wo = sb("wo", [P, D])
        wxc = sb("wxc", [P, CE])
        woc = sb("woc", [P, CE])
        toep = sb("toep", [P, NG, 3 * P])
        w1 = sb("w1", [P, E, F])
        w1f = sb("w1f", [P, F])
        w1h = sb("w1h", [P, E * F], f16)
        w1l = sb("w1l", [P, E * F], f16)
        w2 = sb("w2", [P, E * FB * D])
        b1s = sb("b1s", [P, E * FB])
        b2 = sb("b2", [E, D])
        b2r = sb("b2r", [E, 2, D])
        b2e = sb("b2e", [E, 3, D], bf16)
        b2p = sb("b2p", [3, E * D], bf16)
        ones3 = sb("ones3", [3, P], bf16)
        gS = sb("gS", [P, E])
        x = sb("x", [P, NT, D])
        xT = sb("xT", [P, NT, P])
        v = sb("v", [P, NT, D])
        xc = sb("xc", [P, NT, E])
        att = sb("att", [P, 4, NB, D])
        attT = sb("attT", [P, 4, NB, P])
        st1 = sb("st1", [P, NT, 6])
        mv1 = sb("mv1", [P, NT, 2])
        rs1 = sb("rs1", [P, NT])
        sq_junk = sb("sq_junk", [P, D])
        sq_junk2 = sb("sq_junk2", [P, D])
        ssq2 = sb("ssq2", [P, NT])
        ssq = sb("ssq", [P, NT])
        rso = sb("rso", [P, NT])
        x1 = sb("x1", [P, NT, ROW])
        ocr = sb("ocr", [P, NT, E])
        lg = sb("lg", [P, NT, E])
        colsum = sb("colsum", [P, 1])
        csum = sb("csum", [E, 1])
        mx = sb("mx", [P, NT])
        key = sb("key", [P, NT, E])
        hot = sb("hot", [P, 4, 2 * GT + 1, E], bf16)
        base = sb("base", [P, 5, E])
        posf = sb("posf", [P, NT, E])
        pos = sb("pos", [P, NT], i32)
        free_i = sb("free_i", [1, E], i32)
        count = sb("count", [1, E])
        cmpt = sb("cmpt", [1, E, NT])
        ntile = sb("ntile", [1, E])
        tend = sb("tend", [1, E])
        skip = sb("skip", [1, E])
        past = sb("past", [1, CAP, E])
        jump = sb("jump", [1, CAP, E])
        ef = sb("ef", [1, CAP])
        rf = sb("rf", [1, CAP])
        etab = sb("etab", [1, CAP], i32)
        rtab = sb("rtab", [1, CAP], i32)
        xg = sb("xg", [P, CAP, ROW])
        xn = sb("xn", [P, 3, D])
        xh = sb("xh", [P, 2, P], f16)
        xl = sb("xl", [P, 2, P], f16)
        h = sb("h", [P, 3, FB, P])
        z = sb("z", [P, 2, D])
        st3 = sb("st3", [P, 2, 6])
        mv3 = sb("mv3", [P, 2, 2])
        sd3 = sb("sd3", [P, 2])
        rs3 = sb("rs3", [P, 2])
        nm3 = sb("nm3", [P, 2])
        zn = sb("zn", [P, 2, D])
        o = sb("o", [P, CAP, D])

        l_cent, l_small, l_wi, l_wo, l_toep = sem("l_cent"), sem("l_small"), sem("l_wi"), sem("l_wo"), sem("l_toep")
        l_x = [sem(f"l_x{q}") for q in range(4)]
        l_w1 = [sem(f"l_w1{q}") for q in range(2)]
        l_w2, l_b2 = sem("l_w2"), sem("l_b2")
        c_pool, c_dve, c_pad, p_b2, s_b2, l_b2p = (sem("c_pool"), sem("c_dve"), sem("c_pad"), sem("p_b2"), sem("s_b2"),
                                                   sem("l_b2p"))
        p_cent, p_wi, p_T, p_w, p_wo, p_woc, p_smallT = (sem("p_cent"), sem("p_wi"), sem("p_T"), sem("p_w"), sem("p_wo"),
                                                        sem("p_woc"), sem("p_smallT"))
        p_gS, p_w1f, p_w1h, p_w1l, p_b1, p_b1s = (sem("p_gS"), sem("p_w1f"), sem("p_w1h"), sem("p_w1l"),
                                                  sem("p_b1"), sem("p_b1s"))
        a_mean, a_st, a_var, a_sd, a_rs = sem("a_mean"), sem("a_st"), sem("a_var"), sem("a_sd"), sem("a_rs")
        a_T, a_Te, a_v, a_ve, a_c, a_ce = (sem("a_T"), sem("a_Te"), sem("a_v"), sem("a_ve"), sem("a_c"), sem("a_ce"))
        a_o, a_sq, a_osd, a_ors, a_x1, a_oc, a_oe = (sem("a_o"), sem("a_sq"), sem("a_osd"), sem("a_ors"),
                                                     sem("a_x1"), sem("a_oc"), sem("a_oe"))
        a_var2, a_sd2, a_row, a_lg = sem("a_var2"), sem("a_sd2"), sem("a_row"), sem("a_lg")
        s_rows, s_pad = sem("s_rows"), sem("s_pad")
        r_key, r_place, r_dve, r_hot, r_rank, r_pos, r_free, r_tab = (sem("r_key"), sem("r_place"), sem("r_dve"), sem("r_hot"), sem("r_rank"), sem("r_pos"),
                                                     sem("r_free"), sem("r_tab"))
        g_x = [sem(f"g_x{i}") for i in range(2)]
        s_out = sem("s_out")
        e_xn, e_xT, e_xh, e_xl, e_h1a, e_h1b, e_ha, e_hb = (
            sem("e_xn"), sem("e_xT"), sem("e_xh"), sem("e_xl"), sem("e_h1a"), sem("e_h1b"),
            sem("e_ha"), sem("e_hb"))
        e_nm = sem("e_nm")
        e_y, e_z, e_st, e_var, e_sd, e_rs, e_zn, e_o = (sem("e_y"), sem("e_z"), sem("e_st"), sem("e_var"),
                                                       sem("e_sd"), sem("e_rs"), sem("e_zn"), sem("e_o"))

        bT = [bank[0], bank[1]]
        bV = [bank[2], bank[3]]
        bC = [bank[4], bank[5]]
        bO = [bank[6], bank[7], bank[2], bank[3]]

        def pair(b):
            return b[:, 0:2 * CE].rearrange("p (t c) -> p t c", c=CE)

        rank = bank[0][:, 0:(GT + 1) * E].rearrange("p (t e) -> p t e", e=E)
        b1_ps = bank[4][:, 0:E * FB]
        psX = [bank[0], bank[1]]
        psHa = [bank[2], bank[3]]
        psHb = [bank[4], bank[5]]
        psY = [bank[6], bank[7]]

        def otiles(n):
            hf, qb, bp = n // 4, (n // 2) % 2, n % 2
            t0 = HALF * hf + qb + 4 * bp
            return t0, t0 + 2

        def gtiles(gr):
            t0 = HALF * (gr // 2) + gr % 2
            return slice(t0, t0 + 7, 2)

        def experts(engine):
            return nc.values_load_multi_w_load_instructions(
                etab[0:1, :], engines=(engine,), min_val=0, max_val=E - 1,
                skip_runtime_bounds_check_because="counts of 0 and more, bounded by the minimum with E - 1")[1]

        block = ctx.enter_context(nc.Block())

        @block.sync
        def _(sp):
            def load_x(q):
                sp.dma_start(x[:, 4 * q:4 * q + 4, :], x_view[:, 4 * q:4 * q + 4, :]).then_inc(l_x[q], 16)

            load_x(0)
            sp.dma_start(wi[:, :], wi_d).then_inc(l_wi, 16)
            load_x(1)
            sp.dma_start(toep[:, :, :], toep_d.rearrange("p (g c) -> p g c", g=NG)).then_inc(l_toep, 16)
            load_x(2)
            sp.dma_start(small[0:E, :], lng_d).then_inc(l_small, 16)
            sp.dma_start(small[E:2 * E, :], lnb_d).then_inc(l_small, 16)
            sp.dma_start(small[2 * E:NR, :], b1_d.rearrange("e (f p) -> (e f) p", p=P)).then_inc(l_small, 16)
            load_x(3)
            sp.dma_start(b2[:, :], b2_d).then_inc(l_b2, 16)
            for q in range(2):
                sp.dma_start(w1[:, 4 * q:4 * q + 4, :], w1_d[4 * q:4 * q + 4].rearrange("e d f -> d e f"))\
                    .then_inc(l_w1[q], 16)
            sp.dma_start(w2[:, :].rearrange("p (e f d) -> p e f d", e=E, f=FB),
                         w2_d.rearrange("e (f p) d -> p e f d", p=P)).then_inc(l_w2, 16)
            sp.wait_ge(p_b2, 5)
            sp.dma_start(b2_dram.rearrange("k e d -> e k d"), b2e[:, :, :]).then_inc(s_b2, 16)
            sp.wait_ge(s_b2, 16)
            sp.dma_start(b2p[:, :], b2_dram.rearrange("k e d -> k (e d)")).then_inc(l_b2p, 16)
            sp.wait_ge(c_pad, 2)
            sp.dma_start(rows_dram[E * REGION:E * REGION + SPARE * P, :].rearrange("(s p) c -> p s c", p=P),
                         pad[:, :, :]).then_inc(s_pad, 16)
            sp.wait_ge(r_free, 1)
            for e in range(E):
                row = sp.value_load(free_i[0:1, e:e + 1], min_val=e * REGION, max_val=e * REGION + T)
                sp.dma_start(rows_dram[bass.ds(row, P), :], pad[:, 0, :]).then_inc(s_pad, 16)
            sp.wait_ge(r_tab, 2)
            sp.wait_ge(s_rows, 16 * NT)
            sp.wait_ge(s_pad, 16 * (E + 1))
            for j in range(CAP):
                row = sp.value_load(rtab[0:1, j:j + 1], min_val=0, max_val=E * REGION + SPARE * P - P)
                if j >= 2:
                    sp.wait_ge(g_x[j % 2], 16 * (j // 2))
                sp.dma_start(xg[:, j, :], rows_dram[bass.ds(row, P), :]).then_inc(g_x[j % 2], 16)

        @block.gpsimd
        def _(pool):
            g = nc.gpsimd
            g.memset(ident[:, :], 0.0).then_inc(c_pool, 1)
            g.memset(before[:, :], 1.0).then_inc(c_pool, 1)
            pool.wait_ge(c_pool, 2)
            g.affine_select(out=ident[:, :], in_=ident[:, :], compare_op=ALU.not_equal, fill=1.0, base=0,
                            pattern=[[-1, P]], channel_multiplier=1).then_inc(c_pool, 1)
            g.affine_select(out=before[:, :], in_=before[:, :], compare_op=ALU.is_gt, fill=0.0, base=0,
                            pattern=[[1, P]], channel_multiplier=-1).then_inc(c_pool, 1)
            g.iota(tile_no[:, :], pattern=[[1, CAP]], base=0, channel_multiplier=0,
                   allow_small_or_imprecise_dtypes=True).then_inc(c_pool, 1)
            g.iota(tile_thr[:, :], pattern=[[P, NT]], base=0, channel_multiplier=0,
                   allow_small_or_imprecise_dtypes=True).then_inc(c_pool, 1)
            g.iota(first_wt[:, :], pattern=[[-1, E]], base=E, channel_multiplier=0,
                   allow_small_or_imprecise_dtypes=True).then_inc(c_pool, 1)
            g.iota(region0[:, :], pattern=[[REGION, E]], base=0, channel_multiplier=0,
                   allow_small_or_imprecise_dtypes=True).then_inc(c_pool, 1)
            g.iota(x1[:, :, ROW - 1].bitcast(i32), pattern=[[P, NT]], base=0, channel_multiplier=1)\
                .then_inc(c_pool, 1)
            g.memset(pad[:, :, 0:ROW - 1], 0.0).then_inc(c_pad, 1)
            g.iota(pad[:, :, ROW - 1].bitcast(i32), pattern=[[0, SPARE]], base=NOWHERE, channel_multiplier=0)\
                .then_inc(c_pad, 1)
            pool.wait_ge(l_b2, 16)
            g.tensor_scalar(b2r[:, 0, :], b2[:, :], S, 1.0, ALU.mult, ALU.mult).then_inc(p_b2, 1)
            pool.wait_ge(p_b2, 1)
            g.tensor_copy(b2e[:, 0, :], b2r[:, 0, :]).then_inc(p_b2, 1)
            pool.wait_ge(p_b2, 2)
            g.tensor_tensor(b2r[:, 1, :], b2r[:, 0, :], b2e[:, 0, :], ALU.subtract).then_inc(p_b2, 1)
            pool.wait_ge(p_b2, 3)
            g.tensor_copy(b2e[:, 1, :], b2r[:, 1, :]).then_inc(p_b2, 1)
            pool.wait_ge(p_b2, 4)
            g.tensor_tensor(b2e[:, 2, :], b2r[:, 1, :], b2e[:, 1, :], ALU.subtract).then_inc(p_b2, 1)
            pool.wait_ge(p_gS, 1)
            for e in range(E):
                if e % 4 == 0:
                    pool.wait_ge(l_w1[e // 4], 16)
                if e:
                    pool.wait_ge(p_w1l, e)
                cols = slice(e * F, (e + 1) * F)
                g.tensor_scalar(w1f[:, :], w1[:, e, :], gS[:, e:e + 1], 1.0, ALU.mult, ALU.mult).then_inc(p_w1f, 1)
                pool.wait_ge(p_w1f, e + 1)
                pool.wait_ge(p_w1h, e + 1)
                g.tensor_tensor(w1l[:, cols], w1f[:, :], w1h[:, cols], ALU.subtract).then_inc(p_w1l, 1)

            for gr in range(4):
                pool.wait_ge(a_mean, 4)
                pool.wait_ge(a_row, gr + 1)
                pool.wait_ge(r_pos, gr + 1)
                for k, t in enumerate(range(NT)[gtiles(gr)]):
                    g.indirect_dma_start(
                        out=rows_dram, out_offset=bass.IndirectOffsetOnAxis(
                            ap=pos[:, 4 * gr + k:4 * gr + k + 1].bitcast(u32), axis=0),
                        in_=x1[:, t, :], in_offset=None).then_inc(s_rows, 16)

            for j in range(CAP):
                pool.wait_ge(e_zn, j + 1)
                g.tensor_tensor(o[:, j, :], zn[:, j % 2, :], xg[:, j, 0:D], ALU.add).then_inc(e_o, 1)
                pool.wait_ge(e_o, j + 1)
                g.indirect_dma_start(out=out_rows, out_offset=bass.IndirectOffsetOnAxis(
                                         ap=xg[:, j, ROW - 1:ROW].bitcast(u32), axis=0),
                                     in_=o[:, j, :], in_offset=None, bounds_check=T - 1, oob_is_err=False)\
                    .then_inc(s_out, 16)
            pool.wait_ge(s_out, 16 * CAP)

        @block.scalar
        def _(act):
            s = nc.scalar
            act.dma_start(cent[:, :], cent_d).then_inc(l_cent, 16)
            act.dma_start(wo[:, :], wo_d).then_inc(l_wo, 16)
            act.wait_ge(c_dve, 4)
            s.activation(sq_junk[:, 0:1], eps_t[:, 0:1], ACT.Sqrt, bias=eps_t[:, 0:1])

            def evac_T(n):
                dst = xT[:, 4 * n:4 * n + 4, :] if n < 4 else attT[:, n - 4, :, :]
                act.wait_ge(a_T, n + 1)
                s.activation(dst, bT[n % 2][:, :].rearrange("p (t c) -> p t c", c=P), ACT.Copy).then_inc(a_Te, 1)

            def sd_1(q):
                act.wait_ge(a_var, 4 * q + 4)
                s.activation(rs1[:, 4 * q:4 * q + 4], mv1[:, 4 * q:4 * q + 4, 1], ACT.Sqrt, bias=eps_t[:, 0:1])\
                    .then_inc(a_sd, 1)

            def evac_C(c):
                act.wait_ge(a_c, c + 1)
                s.activation(att[:, c, :, :], bC[c % 2][:, :].rearrange("p (b d) -> p b d", d=D), ACT.Copy)\
                    .then_inc(a_ce, 1)

            def o_stats(n):
                act.wait_ge(a_o, n + 1)
                for k, t in enumerate(otiles(n)):
                    if 2 * n + k:
                        act.wait_ge(a_sq, 2 * n + k)
                    s.activation(sq_junk[:, :], pair(bO[n % 4])[:, k, 0:D], ACT.Square, accum_out=ssq[:, t:t + 1])\
                        .then_inc(a_sq, 1)
                t0, t1 = otiles(n)
                act.wait_ge(a_sq, 2 * n + 2)
                s.activation(rso[:, t0:t1 + 1:2], ssq[:, t0:t1 + 1:2], ACT.Sqrt, bias=eps_t[:, 0:1], scale=1.0 / D)\
                    .then_inc(a_osd, 1)

            def x1_var(n):
                act.wait_ge(a_x1, 2 * n + 2)
                for k, t in enumerate(otiles(n)):
                    if 2 * n + k:
                        act.wait_ge(a_var2, 2 * n + k)
                    s.activation(sq_junk2[:, :], x1[:, t, 0:D], ACT.Square, bias=mv1[:, t, 0:1], scale=-1.0,
                                 accum_out=ssq2[:, t:t + 1]).then_inc(a_var2, 1)

            def sd_2(gr):
                t0 = HALF * (gr // 2) + gr % 2
                act.wait_ge(a_var2, 4 * gr + 4)
                var = ssq2[:, t0:t0 + 7:2]
                s.activation(x1[:, t0:t0 + 7:2, D + 2], var, ACT.Sqrt, bias=eps_t[:, 1:2], scale=1.0 / (D * S ** 2))\
                    .then_inc(a_sd2, 1)
                s.activation(x1[:, t0:t0 + 7:2, D + 1], var, ACT.Sqrt, bias=eps_t[:, 2:3], scale=(1.0 + EPS) / D)\
                    .then_inc(a_sd2, 1)

            def w1_high(e):
                act.wait_ge(l_w1[e // 4], 16)
                act.wait_ge(p_gS, 1)
                s.activation(w1h[:, e * F:(e + 1) * F], w1[:, e, :], ACT.Copy, scale=gS[:, e:e + 1])\
                    .then_inc(p_w1h, 1)

            evac_T(0)
            sd_1(0)
            evac_T(1)
            sd_1(1)
            evac_T(2)
            sd_1(2)
            evac_T(3)
            sd_1(3)
            for e in range(2):
                w1_high(e)
            evac_C(0)
            for e in range(2, 4):
                w1_high(e)
            evac_C(1)
            evac_T(4)
            evac_T(5)
            for e in range(4, 6):
                w1_high(e)
            evac_C(2)
            evac_C(3)
            evac_T(6)
            evac_T(7)
            for n in range(8):
                o_stats(n)
                if n < 2:
                    w1_high(6 + n)
                if n:
                    x1_var(n - 1)
                if n in (2, 4, 6):
                    sd_2(n // 2 - 1)
            x1_var(7)
            sd_2(3)

            def high(j):
                act.wait_ge(e_xT, j + 1)
                if j >= 2:
                    act.wait_ge(e_h1b, j - 1)
                s.activation(xh[:, j % 2, :], psX[j % 2][:, 0:P], ACT.Copy).then_inc(e_xh, 1)

            def hidden_a(j):
                act.wait_ge(e_h1a, j + 1)
                if j >= 3:
                    act.wait_ge(e_y, j - 2)
                for f in range(3):
                    last = s.activation(h[:, j % 3, f, :], psHa[j % 2][:, f * P:(f + 1) * P], ACT.Relu,
                                        bias=b1s[:, bass.ds(expert[j] * FB + f, 1)])
                last.then_inc(e_ha, 1)

            def sd_3(j):
                act.wait_ge(e_var, j + 1)
                s.activation(sd3[:, j % 2:j % 2 + 1], mv3[:, j % 2, 1:2], ACT.Sqrt, bias=eps_t[:, 3:4])\
                    .then_inc(e_sd, 1)

            def normalised(j):
                act.wait_ge(e_nm, j + 1)
                if j >= 2:
                    act.wait_ge(e_o, j - 1)
                s.activation(zn[:, j % 2, :], z[:, j % 2, :], ACT.Identity, scale=rs3[:, j % 2:j % 2 + 1],
                             bias=nm3[:, j % 2:j % 2 + 1]).then_inc(e_zn, 1)

            act.wait_ge(r_tab, 1)
            expert = experts(mybir.EngineType.Activation)
            act.wait_ge(p_b1s, 1)
            high(0)
            for j in range(CAP + 4):
                if 1 <= j <= CAP:
                    hidden_a(j - 1)
                if j + 1 < CAP:
                    high(j + 1)
                if 4 <= j:
                    normalised(j - 4)
                if 3 <= j < CAP + 3:
                    sd_3(j - 3)

        @block.vector
        def _(dve):
            d = nc.vector
            for k, value in enumerate((EPS, EPS / S ** 2, EPS ** 2, EPS * S ** 2)):
                d.memset(eps_t[:, k:k + 1], value).then_inc(c_dve, 1)
            d.memset(ones3[:, :], 1.0).then_inc(c_dve, 1)
            d.memset(ones_bf[:, :], 1.0).then_inc(c_dve, 1)
            d.memset(ones_e[:, :], 1.0).then_inc(c_dve, 1)
            d.memset(hot[:, :, :], 0.0).then_inc(c_dve, 1)

            def x_rstd(q):
                dve.wait_ge(a_sd, q + 1)
                d.reciprocal(rs1[:, 4 * q:4 * q + 4], rs1[:, 4 * q:4 * q + 4]).then_inc(a_rs, 1)
                dve.wait_ge(a_var, 4 * q + 4)
                d.tensor_copy(x1[:, 4 * q:4 * q + 4, D], mv1[:, 4 * q:4 * q + 4, 0]).then_inc(a_mean, 1)

            def x_stat(t):
                if t % 4 == 0:
                    dve.wait_ge(l_x[t // 4], 16)
                d.bn_stats(st1[:, t, :], x[:, t, :]).then_inc(a_st, 1)

            def x_var(q):
                for t in range(4 * q, 4 * q + 4):
                    dve.wait_ge(a_st, t + 1)
                    d.bn_aggr(mv1[:, t, :], st1[:, t, :]).then_inc(a_var, 1)

            dve.wait_ge(l_cent, 16)
            d.reduce_sum(csum[:, :], cent[:, :], AX.X).then_inc(p_cent, 1)
            x_stat(0)
            dve.wait_ge(p_cent, 1)
            d.tensor_scalar(csum[:, :], csum[:, :], -1.0 / D, None, ALU.mult).then_inc(p_cent, 1)
            x_stat(1)
            dve.wait_ge(p_cent, 2)
            d.tensor_scalar(cent[:, :], cent[:, :], csum[:, 0:1], None, ALU.add).then_inc(p_cent, 1)
            dve.wait_ge(l_wi, 16)
            d.reduce_sum(colsum[:, :], wi[:, :], AX.X).then_inc(p_wi, 1)
            x_stat(2)
            dve.wait_ge(p_wi, 1)
            d.tensor_scalar(colsum[:, :], colsum[:, :], -1.0 / D, None, ALU.mult).then_inc(p_wi, 1)
            x_stat(3)
            dve.wait_ge(p_wi, 2)
            d.tensor_scalar(wi[:, :], wi[:, :], colsum[:, 0:1], None, ALU.add).then_inc(p_wi, 1)
            dve.wait_ge(c_pool, 3)
            d.tensor_scalar(centring[:, 0:D], ident[:, :], -1.0 / D, None, ALU.add).then_inc(p_wo, 1)
            dve.wait_ge(p_T, 1)
            d.tensor_copy(wxc[:, D:CE], bank[7][:, 0:E]).then_inc(p_w, 1)
            d.tensor_copy(centring[:, D:CE], bank[7][:, 0:E]).then_inc(p_wo, 1)
            dve.wait_ge(p_T, 2)
            d.tensor_copy(wxc[:, 0:D], bank[6][:, 0:P]).then_inc(p_w, 1)

            def other_parameters():
                dve.wait_ge(p_T, 3)
                d.tensor_copy(woc[:, :], bank[5][:, 0:CE]).then_inc(p_woc, 1)
                dve.wait_ge(p_T, 4)
                d.tensor_copy(smallT[:, :], bank[4][:, 0:NR]).then_inc(p_smallT, 1)
                dve.wait_ge(p_smallT, 1)
                d.tensor_scalar(gS[:, :], smallT[:, 0:E], S, None, ALU.mult).then_inc(p_gS, 1)

            def values(n):
                dve.wait_ge(a_v, n + 1)
                t0 = 2 * n
                if n % 2 == 0:
                    dve.wait_ge(a_rs, n // 2 + 1)
                src = pair(bV[n % 2])
                d.tensor_tensor(v[:, t0:t0 + 2, :], src[:, :, 0:D],
                                rs1[:, t0:t0 + 2].unsqueeze(2).broadcast_to([P, 2, D]), ALU.mult)
                d.tensor_copy(xc[:, t0:t0 + 2, :], src[:, :, D:CE]).then_inc(a_ve, 1)

            def row_rstd(gr):
                t0 = HALF * (gr // 2) + gr % 2
                dve.wait_ge(a_sd2, 2 * gr + 2)
                d.reciprocal(x1[:, t0:t0 + 7:2, D + 1:D + 3], x1[:, t0:t0 + 7:2, D + 1:D + 3]).then_inc(a_row, 1)

            def over_e(a):
                return a.unsqueeze(2).broadcast_to([P, GT, E])

            def over_t(a):
                return a.unsqueeze(1).broadcast_to([P, GT, E])

            def choose(gr, step):
                logit, k, m = lg[:, gtiles(gr), :], key[:, 4 * gr:4 * gr + 4, :], mx[:, 4 * gr:4 * gr + 4]
                if step:
                    dve.wait_ge(r_key, 4 * gr + step)
                if step == 0:
                    dve.wait_ge(a_lg, 2 * gr + 2)
                    d.reduce_max(m, logit, AX.X).then_inc(r_key, 1)
                elif step == 1:
                    d.tensor_tensor(k, logit, over_e(m), ALU.is_equal).then_inc(r_key, 1)
                elif step == 2:
                    d.tensor_tensor(k, k, over_t(first_wt[:, :]), ALU.mult).then_inc(r_key, 1)
                elif step == 3:
                    d.reduce_max(m, k, AX.X).then_inc(r_key, 1)
                else:
                    d.tensor_tensor(hot[:, gr, GT:2 * GT, :], k, over_e(m), ALU.is_equal).then_inc(r_hot, 1)

            def place(gr, step):
                f, m = posf[:, 4 * gr:4 * gr + 4, :], mx[:, 4 * gr:4 * gr + 4]
                if step >= 2:
                    dve.wait_ge(r_place, 4 * gr + step)
                if step == 0:
                    dve.wait_ge(r_rank, gr + 1)
                    if gr:
                        dve.wait_ge(r_place, 4 * gr - 2)
                    d.tensor_tensor(f, rank[:, 0:GT, :], over_t(base[:, gr, :]), ALU.add).then_inc(r_place, 1)
                elif step == 1:
                    d.tensor_tensor(base[:, gr + 1, :], rank[:, GT, :], base[:, gr, :], ALU.add).then_inc(r_place, 1)
                elif step == 2:
                    d.tensor_tensor(f, f, hot[:, gr, GT:2 * GT, :], ALU.mult).then_inc(r_place, 1)
                elif step == 3:
                    d.reduce_sum(m, f, AX.X).then_inc(r_place, 1)
                else:
                    d.tensor_copy(pos[:, 4 * gr:4 * gr + 4], m).then_inc(r_pos, 1)

            def no_route(step):
                pass

            def residual(n, route):
                t0, t1 = otiles(n)
                two = slice(t0, t1 + 1, 2)
                dve.wait_ge(a_osd, n + 1)
                d.reciprocal(rso[:, two], rso[:, two]).then_inc(a_ors, 1)
                route(0)
                dve.wait_ge(a_ors, n + 1)
                src = pair(bO[n % 4])
                route(1)
                d.tensor_tensor(ocr[:, two, :], src[:, :, D:CE], rso[:, two].unsqueeze(2).broadcast_to([P, 2, E]),
                                ALU.mult).then_inc(a_oe, 1)
                for k, t in enumerate((t0, t1)):
                    d.scalar_tensor_tensor(x1[:, t, 0:D], src[:, k, 0:D], rso[:, t:t + 1], x[:, t, :],
                                           ALU.mult, ALU.add).then_inc(a_x1, 1)
                    route(2 + k)
                dve.wait_ge(a_oe, n + 1)
                d.tensor_tensor(lg[:, two, :], ocr[:, two, :], xc[:, two, :], ALU.add).then_inc(a_lg, 1)
                route(4)

            def x_stats(q):
                for t in range(4 * q, 4 * q + 4):
                    x_stat(t)
                x_var(q)

            x_var(0)
            x_stats(1)
            x_rstd(0)
            values(0)
            values(1)
            x_rstd(1)
            values(2)
            values(3)
            other_parameters()
            x_stats(2)
            x_stats(3)
            x_rstd(2)
            x_rstd(3)
            for n in range(4, 8):
                values(n)
            dve.wait_ge(c_pool, 9)
            dve.wait_ge(c_dve, 8)
            d.tensor_copy(base[:, 0, :], region0[:, :]).then_inc(r_dve, 1)
            dve.wait_ge(r_dve, 1)
            residual(0, no_route)
            residual(1, no_route)
            for gr in range(3):
                residual(2 * gr + 2, lambda step: choose(gr, step))
                row_rstd(gr)
                residual(2 * gr + 3, lambda step: place(gr, step))
            for step in range(5):
                choose(3, step)
            row_rstd(3)
            for step in range(5):
                place(3, step)
            links = [1]

            def link(ins):
                links[0] += 1
                ins.then_inc(r_dve, 1)
                dve.wait_ge(r_dve, links[0])

            d.tensor_copy(free_i[:, :], base[0:1, 4, :]).then_inc(r_free, 1)
            link(d.tensor_tensor(count[:, :], base[0:1, 4, :], region0[0:1, :], ALU.subtract))
            link(d.tensor_tensor(cmpt[:, :, :], count[:, :].unsqueeze(2).broadcast_to([1, E, NT]),
                                 tile_thr[0:1, :].unsqueeze(1).broadcast_to([1, E, NT]), ALU.is_gt))
            link(d.reduce_sum(ntile[:, :], cmpt[:, :, :], AX.X))
            link(d.tensor_tensor_scan(tend[:, :], ones_e[0:1, :], ntile[:, :], 0.0, ALU.mult, ALU.add))
            link(d.tensor_tensor(past[:, :, :], tend[:, :].unsqueeze(1).broadcast_to([1, CAP, E]),
                                 tile_no[:, :].unsqueeze(2).broadcast_to([1, CAP, E]), ALU.is_le))
            link(d.reduce_sum(ef[:, :], past[:, :, :], AX.X))
            d.tensor_scalar(etab[:, :], ef[:, :], float(E - 1), None, ALU.min).then_inc(r_tab, 1)
            link(d.tensor_scalar(skip[:, :], ntile[:, :], -float(P), float(REGION), ALU.mult, ALU.add))
            link(d.tensor_tensor(jump[:, :, :], past[:, :, :], skip[:, :].unsqueeze(1).broadcast_to([1, CAP, E]),
                                 ALU.mult))
            link(d.reduce_sum(rf[:, :], jump[:, :, :], AX.X))
            d.scalar_tensor_tensor(rtab[:, :], tile_no[:, :], float(P), rf[:, :], ALU.mult, ALU.add)\
                .then_inc(r_tab, 1)
            dve.wait_ge(p_b1, E)
            link(d.tensor_tensor(b1s[:, :], b1_ps, smallT[:, 2 * E:NR], ALU.add))
            d.tensor_scalar(b1s[:, :], b1s[:, :], S, None, ALU.mult).then_inc(p_b1s, 1)

            def norm(j):
                dve.wait_ge(g_x[j % 2], 16 * (j // 2 + 1))
                if j >= 3:
                    dve.wait_ge(e_xT, j - 2)
                d.tensor_scalar(xn[:, j % 3, :], xg[:, j, 0:D], xg[:, j, D:D + 1], xg[:, j, D + 1:D + 2],
                                ALU.subtract, ALU.mult).then_inc(e_xn, 1)

            def low(j):
                dve.wait_ge(e_xh, j + 1)
                d.tensor_tensor(xl[:, j % 2, :], psX[j % 2][:, 0:P], xh[:, j % 2, :], ALU.subtract)\
                    .then_inc(e_xl, 1)

            def hidden_b(j):
                dve.wait_ge(e_h1b, j + 1)
                if j >= 3:
                    dve.wait_ge(e_y, j - 2)
                d.tensor_scalar(h[:, j % 3, 3, :], psHb[j % 2][:, 0:P], b1s[:, bass.ds(expert[j] * FB + 3, 1)], 0.0,
                                ALU.add, ALU.max).then_inc(e_hb, 1)

            def output_sum(j):
                dve.wait_ge(e_y, j + 1)
                if j >= 2:
                    dve.wait_ge(e_zn, j - 1)
                d.scalar_tensor_tensor(z[:, j % 2, :], xg[:, j, 0:D], xg[:, j, D + 2:D + 3], psY[j % 2][:, 0:D],
                                       ALU.mult, ALU.add).then_inc(e_z, 1)

            def output_stats(j):
                dve.wait_ge(e_z, j + 1)
                d.bn_stats(st3[:, j % 2, :], z[:, j % 2, :]).then_inc(e_st, 1)

            def output_var(j):
                dve.wait_ge(e_st, j + 1)
                d.bn_aggr(mv3[:, j % 2, :], st3[:, j % 2, :]).then_inc(e_var, 1)

            def output_rstd(j):
                dve.wait_ge(e_sd, j + 1)
                d.reciprocal(rs3[:, j % 2:j % 2 + 1], sd3[:, j % 2:j % 2 + 1]).then_inc(e_rs, 1)

            def output_shift(j):
                dve.wait_ge(e_rs, j + 1)
                d.tensor_scalar(nm3[:, j % 2:j % 2 + 1], mv3[:, j % 2, 0:1], rs3[:, j % 2:j % 2 + 1], -1.0,
                                ALU.mult, ALU.mult).then_inc(e_nm, 1)

            dve.wait_ge(r_tab, 1)
            expert = experts(mybir.EngineType.DVE)
            norm(0)
            norm(1)
            low(0)
            for j in range(CAP + 4):
                if j >= 4:
                    output_rstd(j - 4)
                if 3 <= j < CAP + 3:
                    output_sum(j - 3)
                if j >= 4:
                    output_shift(j - 4)
                if j + 2 < CAP:
                    norm(j + 2)
                if 3 <= j < CAP + 3:
                    output_stats(j - 3)
                if 1 <= j <= CAP:
                    hidden_b(j - 1)
                if 3 <= j < CAP + 3:
                    output_var(j - 3)
                if j + 1 < CAP:
                    low(j + 1)

        @block.tensor
        def _(pe):
            t_ = nc.tensor

            def transposes(n, src, done):
                if n >= 2:
                    pe.wait_ge(a_Te, n - 1)
                for k in range(4):
                    last = t_.transpose(bT[n % 2][:, k * P:(k + 1) * P], src[k], ident[:, :])
                last.then_inc(done, 1)

            def x_T(q):
                pe.wait_ge(l_x[q], 16)
                transposes(q, [x[:, 4 * q + k, :] for k in range(4)], a_T)

            def att_T(n):
                pe.wait_ge(a_ce, n - 3)
                transposes(n, [att[:, n - 4, k, :] for k in range(4)], a_T)

            def project_x(n):
                if n % 2 == 0:
                    pe.wait_ge(a_Te, n // 2 + 1)
                if n >= 2:
                    pe.wait_ge(a_ve, n - 1)
                for k in range(2):
                    last = t_.matmul(pair(bV[n % 2])[:, k, :], xT[:, 2 * n + k, :], wxc[:, :], start=True, stop=True)
                last.then_inc(a_v, 1)

            def attend(c):
                hf, qb = c // 2, c % 2
                if c >= 1:
                    pe.wait_ge(a_ce, c - 1)
                dst = bC[c % 2][:, :].rearrange("p (b u g i) -> p b u g i", b=NB, u=2, g=NG)
                val = v[:, HALF * hf:HALF * (hf + 1), :].rearrange("p (b k) (u g i) -> p k b u g i", k=2, u=2, g=NG)
                for g in range(NG):
                    for kb in range(2):
                        off = P * (1 - kb + qb)
                        last = t_.matmul(dst[:, :, :, g, :], toep[:, g, off:off + P], val[:, kb, :, :, g, :],
                                         start=(kb == 0), stop=(kb == 1))
                last.then_inc(a_c, 1)

            def project_o(n):
                if n % 2 == 0:
                    pe.wait_ge(a_Te, n // 2 + 5)
                if n >= 4:
                    pe.wait_ge(a_x1, 2 * (n - 3))
                    pe.wait_ge(a_oe, n - 3)
                elif n >= 2:
                    pe.wait_ge(a_ve, 8)
                for k in range(2):
                    last = t_.matmul(pair(bO[n % 4])[:, k, :], attT[:, n // 2, 2 * (n % 2) + k, :], woc[:, :],
                                     start=True, stop=True)
                last.then_inc(a_o, 1)

            def ln_b_w1(e):
                if e == 0:
                    pe.wait_ge(a_ce, 4)
                    pe.wait_ge(p_smallT, 1)
                pe.wait_ge(l_w1[e // 4], 16)
                for f in range(FB):
                    last = t_.matmul(b1_ps[:, e * FB + f:e * FB + f + 1], w1[:, e, f * P:(f + 1) * P],
                                     smallT[:, E + e:E + e + 1], start=True, stop=True)
                last.then_inc(p_b1, 1)

            pe.wait_ge(c_pool, 3)
            x_T(0)
            pe.wait_ge(p_cent, 3)
            t_.transpose(bank[7][:, 0:E], cent[:, :], ident[0:E, 0:E]).then_inc(p_T, 1)
            pe.wait_ge(p_wi, 3)
            t_.transpose(bank[6][:, 0:P], wi[:, :], ident[:, :]).then_inc(p_T, 1)
            x_T(1)
            pe.wait_ge(p_wo, 2)
            pe.wait_ge(l_wo, 16)
            t_.matmul(bank[5][:, 0:CE], wo[:, :], centring[:, :], start=True, stop=True).then_inc(p_T, 1)
            pe.wait_ge(p_w, 2)
            for n in range(4):
                project_x(n)
            pe.wait_ge(l_small, 48)
            t_.transpose(bank[4][:, 0:NR], small[:, :], ident[0:NR, 0:NR]).then_inc(p_T, 1)
            x_T(2)
            x_T(3)
            pe.wait_ge(l_toep, 16)
            pe.wait_ge(a_ve, 4)
            pe.wait_ge(p_woc, 1)
            pe.wait_ge(p_smallT, 1)
            attend(0)
            attend(1)
            for n in range(4, 8):
                project_x(n)
            att_T(4)
            att_T(5)
            pe.wait_ge(a_ve, 8)
            attend(2)
            attend(3)
            att_T(6)
            att_T(7)

            def ranks(gr):
                pe.wait_ge(r_hot, gr + 1)
                if gr:
                    pe.wait_ge(r_pos, gr)
                else:
                    pe.wait_ge(c_pool, 4)
                    pe.wait_ge(c_dve, 8)
                    pe.wait_ge(a_Te, 8)
                for k in range(GT, 0, -1):
                    t_.matmul(rank[:, :, :], ones_bf[:, :], hot[:, gr, GT - k:2 * GT + 1 - k, :],
                              start=(k == GT), stop=False)
                t_.matmul(rank[:, :, :], before[:, :], hot[:, gr, GT:2 * GT + 1, :], start=False, stop=True)\
                    .then_inc(r_rank, 1)

            for n in range(8):
                project_o(n)
                if n in (4, 6):
                    ranks(n // 2 - 2)
            ranks(2)
            ranks(3)
            for e in range(E):
                ln_b_w1(e)

            def input_T(j):
                pe.wait_ge(e_xn, j + 1)
                if j >= 2:
                    pe.wait_ge(e_xl, j - 1)
                t_.transpose(psX[j % 2][:, 0:P], xn[:, j % 3, :], ident[:, :]).then_inc(e_xT, 1)

            def up(j, f):
                if f == 0:
                    pe.wait_ge(e_xl, j + 1)
                    if j >= 2:
                        pe.wait_ge(e_ha, j - 1)
                        pe.wait_ge(e_hb, j - 1)
                dst = (psHa[j % 2][:, f * P:(f + 1) * P] if f < 3 else psHb[j % 2][:, 0:P])
                cols = bass.ds(expert[j] * F + f * P, P)
                t_.matmul(dst, w1h[:, cols], xh[:, j % 2, :], start=True, stop=False)
                t_.matmul(dst, w1h[:, cols], xl[:, j % 2, :], start=False, stop=False)
                last = t_.matmul(dst, w1l[:, cols], xh[:, j % 2, :], start=False, stop=True)
                if f >= 2:
                    last.then_inc((e_h1a, e_h1b)[f - 2], 1)

            def down(j, f):
                y = psY[j % 2][:, 0:D]
                if f == 0:
                    pe.wait_ge(e_ha, j + 1)
                    pe.wait_ge(e_hb, j + 1)
                    if j >= 2:
                        pe.wait_ge(e_z, j - 1)
                    t_.matmul(y, ones3[:, :], b2p[:, bass.ds(expert[j] * D, D)], start=True, stop=False)
                last = t_.matmul(y, h[:, j % 3, f, :], w2[:, bass.ds(expert[j] * (FB * D) + f * D, D)],
                                 start=False, stop=(f == FB - 1))
                if f == FB - 1:
                    last.then_inc(e_y, 1)

            pe.wait_ge(r_tab, 1)
            expert = experts(mybir.EngineType.PE)
            pe.wait_ge(p_w1l, E)
            pe.wait_ge(l_w2, 16)
            pe.wait_ge(l_b2p, 16)
            input_T(0)
            for j in range(CAP + 2):
                if j + 1 < CAP:
                    input_T(j + 1)
                for f in range(FB):
                    if j < CAP:
                        up(j, f)
                    if j >= 2:
                        down(j - 2, f)


_INS = ['L0_attn_values', 'L0_attn_input_weights', 'L0_attn_output_weight', 'L0_ffn_centroids', 'L0_ffn_ln_g',
        'L0_ffn_ln_b', 'L0_ffn_W1', 'L0_ffn_b1', 'L0_ffn_W2', 'L0_ffn_b2']


def toeplitz_table(np):
    dist = (np.arange(128)[:, None] - np.arange(384)[None, :] + 128).astype(np.float32)
    parts = []
    for std, off in zip(ATTN_STD, ATTN_OFFSET):
        std, off = np.float32(std), np.float32(off)
        norm = np.float32(1.0 / (float(std) * np.sqrt(2.0 * np.pi)))
        parts.append(norm * np.exp(np.float32(-0.5) * ((dist - off) / std) ** 2))
    return np.stack(parts, 1).reshape(128, -1).astype(np.float32)


def kernel(**inputs):
    import numpy as _np
    import concourse.bacc as _bacc
    from concourse import mybir as _mybir
    from concourse.bass_utils import run_bass_kernel_spmd as _run

    nc = _bacc.Bacc("TRN2", target_bir_lowering=False, num_devices=1)
    arrays, args = {}, []
    for name in _INS:
        a = _np.ascontiguousarray(inputs[name])
        arrays[f"in_{name}_dram"] = a
        args.append(nc.dram_tensor(f"in_{name}_dram", a.shape, _mybir.dt.from_np(a.dtype), kind="ExternalInput").ap())
    table = toeplitz_table(_np)
    arrays["in_toeplitz_dram"] = table
    args.append(nc.dram_tensor("in_toeplitz_dram", table.shape, _mybir.dt.float32, kind="ExternalInput").ap())
    shape = inputs['L0_attn_values'].shape
    args.append(nc.dram_tensor("out_0_dram", shape, _mybir.dt.float32, kind="ExternalOutput").ap())
    attention_moe_block(nc, *args)
    r = _run(nc, [arrays], core_ids=[0])
    return r.results[0]["out_0_dram"]
```

```python
import concourse.bass as bass
from concourse import mybir
from contextlib import ExitStack

ATTN_STD = (1.0, 2.0, 4.0, 8.0)
ATTN_OFFSET = (-1.0, -2.0, -4.0, -8.0)


def attention_moe_block(nc, x_d, wi_d, wo_d, cent_d, lng_d, lnb_d, w1_d, b1_d, w2_d, b2_d, toep_d, out_d):
    fp32, bf16, f16, i32 = mybir.dt.float32, mybir.dt.bfloat16, mybir.dt.float16, mybir.dt.int32
    u32 = mybir.dt.uint32
    ALU, ACT, AX = mybir.AluOpType, mybir.ActivationFunctionType, mybir.AxisListType

    P = 128
    B, L, D = x_d.shape
    E, _, F = w1_d.shape
    T = B * L
    NT = T // P
    FB = F // P
    CAP = NT + E - 1
    NG = len(ATTN_STD)
    HD = D // (2 * NG)
    HALF = NT // 2
    NB = HALF // 2
    EPS = 1e-5
    S = 64.0
    ROW = D + 4
    CE = D + E
    NR = 2 * E + FB * E

    REGION = T + P
    SPARE = CAP - NT
    NOWHERE = 2 * T
    LAST = 3
    GT = 4
    rows_dram = nc.dram_tensor("expert_rows", [E * REGION + SPARE * P, ROW], fp32, kind="Internal").ap()
    b2_dram = nc.dram_tensor("b2_parts", [3, E, D], bf16, kind="Internal").ap()
    x_view = x_d.rearrange("b l d -> (b l) d").rearrange("(t p) d -> p t d", p=P)
    out_rows = out_d.rearrange("b l d -> (b l) d")

    ctx = ExitStack()
    with ctx:
        def sb(name, shape, dt=fp32):
            return ctx.enter_context(nc.sbuf_tensor(name, shape, dt))

        def sem(name):
            return ctx.enter_context(nc.semaphore(name))

        bank = [ctx.enter_context(nc.psum_tensor(f"bank{i}", [P, 512], fp32)) for i in range(8)]

        ident = sb("ident", [P, P])
        ones_bf = sb("ones_bf", [P, P], bf16)
        before = sb("before", [P, P], bf16)
        tile_no = sb("tile_no", [1, CAP])
        tile_thr = sb("tile_thr", [P, NT])
        first_wt = sb("first_wt", [P, E])
        region0 = sb("region0", [P, E])
        pad = sb("pad", [P, SPARE, ROW])
        ones_e = sb("ones_e", [P, E])
        eps_t = sb("eps_t", [P, 4])
        cent = sb("cent", [E, D])
        small = sb("small", [NR, D])
        smallT = sb("smallT", [P, NR])
        centring = sb("centring", [P, CE])
        wi = sb("wi", [P, D])
        wo = sb("wo", [P, D])
        wxc = sb("wxc", [P, CE])
        woc = sb("woc", [P, CE])
        toep = sb("toep", [P, NG, 3 * P])
        w1 = sb("w1", [P, E, F])
        w1s = sb("w1s", [P, E * F])
        w1p = w1s[:, :].bitcast(f16).rearrange("p (e f k c) -> p e f k c", e=E, f=FB, k=2)
        w2 = sb("w2", [P, E * FB * D])
        b1s = sb("b1s", [P, E * FB])
        b2 = sb("b2", [E, D])
        b2r = sb("b2r", [E, 2, D])
        b2e = sb("b2e", [E, 3, D], bf16)
        b2p = sb("b2p", [3, 2 * E * F], bf16)
        ones3 = sb("ones3", [3, P], bf16)
        gS = sb("gS", [P, E])
        x = sb("x", [P, NT, D])
        xT = sb("xT", [P, NT, P])
        v = sb("v", [P, NT, D])
        xc = sb("xc", [P, NT, E])
        att = sb("att", [P, 4, NB, D])
        attT = sb("attT", [P, 4, NB, P])
        st1 = sb("st1", [P, NT, 6])
        mv1 = sb("mv1", [P, NT, 2])
        rs1 = sb("rs1", [P, NT])
        warm = sb("warm", [P, 1])
        ssq2 = sb("ssq2", [P, NT])
        ssq = sb("ssq", [P, NT])
        rso = sb("rso", [P, NT])
        x1 = sb("x1", [P, NT, ROW])
        ocr = sb("ocr", [P, NT, E])
        lg = sb("lg", [P, NT, E])
        colsum = sb("colsum", [P, 1])
        csum = sb("csum", [E, 1])
        mx = sb("mx", [P, NT])
        key = sb("key", [P, NT, E])
        hot = sb("hot", [P, 4, 2 * GT + 1, E], bf16)
        base = sb("base", [P, 5, E])
        posf = sb("posf", [P, NT, E])
        pos = sb("pos", [P, NT], i32)
        free_i = sb("free_i", [1, E], i32)
        count = sb("count", [1, E])
        cmpt = sb("cmpt", [1, E, NT])
        ntile = sb("ntile", [1, E])
        tend = sb("tend", [1, E])
        skip = sb("skip", [1, E])
        past = sb("past", [1, CAP, E])
        jump = sb("jump", [1, CAP, E])
        ef = sb("ef", [1, CAP])
        rf = sb("rf", [1, CAP])
        etab = sb("etab", [1, CAP], i32)
        rtab = sb("rtab", [1, CAP], i32)
        xg = sb("xg", [P, CAP, ROW])
        xn = sb("xn", [P, 3, D])
        xh = sb("xh", [P, 2, P], f16)
        xl = sb("xl", [P, 2, P], f16)
        h = sb("h", [P, 3, FB, P])
        z = sb("z", [P, 2, D])
        st3 = sb("st3", [P, 2, 6])
        mv3 = sb("mv3", [P, 2, 2])
        sd3 = sb("sd3", [P, 2])
        rs3 = sb("rs3", [P, 2])
        nm3 = sb("nm3", [P, 2])
        zn = sb("zn", [P, 2, D])
        o = sb("o", [P, CAP, D])

        l_cent, l_small, l_wi, l_wo, l_toep = sem("l_cent"), sem("l_small"), sem("l_wi"), sem("l_wo"), sem("l_toep")
        l_x = [sem(f"l_x{q}") for q in range(4)]
        l_w1 = [sem(f"l_w1{q}") for q in range(2)]
        l_w2, l_b2, l_b2p = sem("l_w2"), sem("l_b2"), sem("l_b2p")
        c_pool, c_dve, c_pad = sem("c_pool"), sem("c_dve"), sem("c_pad")
        p_b2, s_b2 = sem("p_b2"), sem("s_b2")
        p_cent, p_wi = sem("p_cent"), sem("p_wi")
        p_T = sem("p_T")
        p_w, p_wo, p_woc = sem("p_w"), sem("p_wo"), sem("p_woc")
        p_smallT, p_gS = sem("p_smallT"), sem("p_gS")
        p_w1h, p_w1l = sem("p_w1h"), sem("p_w1l")
        p_b1, p_b1s = sem("p_b1"), sem("p_b1s")
        a_st, a_var, a_sd, a_rs = sem("a_st"), sem("a_var"), sem("a_sd"), sem("a_rs")
        a_mean = sem("a_mean")
        a_T, a_Te = sem("a_T"), sem("a_Te")
        a_v = sem("a_v")
        a_vs, a_ve = sem("a_vs"), sem("a_ve")
        a_c, a_ce = sem("a_c"), sem("a_ce")
        a_o = sem("a_o")
        a_sq, a_osd, a_ors = sem("a_sq"), sem("a_osd"), sem("a_ors")
        a_oe, a_x1, a_lg = sem("a_oe"), sem("a_x1"), sem("a_lg")
        a_var2, a_var2d = sem("a_var2"), sem("a_var2d")
        a_sd2, a_row = sem("a_sd2"), sem("a_row")
        r_key, r_hot = sem("r_key"), sem("r_hot")
        r_rank = sem("r_rank")
        r_place, r_pos = sem("r_place"), sem("r_pos")
        r_dve, r_free, r_tab = sem("r_dve"), sem("r_free"), sem("r_tab")
        s_rows, s_pad = sem("s_rows"), sem("s_pad")
        g_x = [sem(f"g_x{i}") for i in range(4)]
        e_xn, e_xT, e_xh, e_xl = sem("e_xn"), sem("e_xT"), sem("e_xh"), sem("e_xl")
        e_h1a, e_h1b = sem("e_h1a"), sem("e_h1b")
        e_ha, e_hb = sem("e_ha"), sem("e_hb")
        e_y, e_z = sem("e_y"), sem("e_z")
        e_st, e_var, e_sd, e_rs, e_nm = sem("e_st"), sem("e_var"), sem("e_sd"), sem("e_rs"), sem("e_nm")
        e_zn, e_zlast = sem("e_zn"), sem("e_zlast")
        e_o, e_olast = sem("e_o"), sem("e_olast")
        s_out = sem("s_out")

        bT = [bank[0], bank[1]]
        bV = [bank[2], bank[3], bank[4], bank[5], bank[2], bank[3], bank[2], bank[3]]
        bC = [bank[4], bank[5]]
        bO = [bank[6], bank[7], bank[2], bank[3]]

        def pair(b):
            return b[:, 0:2 * CE].rearrange("p (t c) -> p t c", c=CE)

        rank = bank[0][:, 0:(GT + 1) * E].rearrange("p (t e) -> p t e", e=E)
        b1_ps = bank[4][:, 0:E * FB]
        psX = [bank[0], bank[1]]
        psHa = [bank[2], bank[3]]
        psHb = [bank[4], bank[5]]
        psY = [bank[6], bank[7]]

        def otiles(n):
            hf, qb, bp = n // 4, (n // 2) % 2, n % 2
            t0 = HALF * hf + qb + 4 * bp
            return t0, t0 + 2

        def gtiles(gr):
            t0 = HALF * (gr // 2) + gr % 2
            return slice(t0, t0 + 7, 2)

        def table_values(table, engine, largest):
            return nc.values_load_multi_w_load_instructions(
                table, engines=(engine,), min_val=0, max_val=largest,
                skip_runtime_bounds_check_because="sums of counts of at most T tokens, cut at the last expert")[1]

        def wait_output(engine, j):
            if j < CAP - LAST:
                engine.wait_ge(e_o, j + 1)
            else:
                engine.wait_ge(e_olast, j - (CAP - LAST) + 1)

        def of_expert(weights, width, offset, first, size):
            last = 4 * (E - 1) * width + first + size
            return weights[:, :].bitcast(mybir.dt.uint8)[:, first:last][:, bass.ds(offset, size)]

        def pad_experts(queue, engine, experts):
            queue.wait_ge(c_pad, 2)
            queue.wait_ge(r_free, 1)
            rows = table_values(free_i[0:1, experts[0]:experts[-1] + 1], engine, (E - 1) * REGION + T)
            for row in rows:
                queue.dma_start(rows_dram[bass.ds(row, P), :], pad[:, 0, :]).then_inc(s_pad, 16)

        block = ctx.enter_context(nc.Block())

        @block.sync
        def _(sp):
            def load_x(q):
                sp.dma_start(x[:, 4 * q:4 * q + 4, :], x_view[:, 4 * q:4 * q + 4, :]).then_inc(l_x[q], 16)

            load_x(0)
            sp.dma_start(wi[:, :], wi_d).then_inc(l_wi, 16)
            load_x(1)
            sp.dma_start(toep[:, :, :], toep_d.rearrange("p (g c) -> p g c", g=NG)).then_inc(l_toep, 16)
            load_x(2)
            sp.dma_start(small[0:E, :], lng_d).then_inc(l_small, 16)
            sp.dma_start(small[E:2 * E, :], lnb_d).then_inc(l_small, 16)
            sp.dma_start(small[2 * E:NR, :], b1_d.rearrange("e (f p) -> (e f) p", p=P)).then_inc(l_small, 16)
            load_x(3)
            sp.dma_start(b2[:, :], b2_d).then_inc(l_b2, 16)
            for q in range(2):
                sp.dma_start(w1[:, 4 * q:4 * q + 4, :], w1_d[4 * q:4 * q + 4].rearrange("e d f -> d e f"))\
                    .then_inc(l_w1[q], 16)
            sp.dma_start(w2[:, :].rearrange("p (e f d) -> p e f d", e=E, f=FB),
                         w2_d.rearrange("e (f p) d -> p e f d", p=P)).then_inc(l_w2, 16)
            sp.wait_ge(p_b2, 5)
            sp.dma_start(b2_dram.rearrange("k e d -> e k d"), b2e[:, :, :]).then_inc(s_b2, 16)
            sp.wait_ge(s_b2, 16)
            sp.dma_start(b2p[:, :].rearrange("k (e c) -> k e c", e=E)[:, :, 0:D], b2_dram).then_inc(l_b2p, 16)
            sp.wait_ge(c_pad, 2)
            sp.dma_start(rows_dram[E * REGION:E * REGION + SPARE * P, :].rearrange("(s p) c -> p s c", p=P),
                         pad[:, :, :]).then_inc(s_pad, 16)
            pad_experts(sp, mybir.EngineType.SP, range(0, E // 2))
            sp.wait_ge(r_tab, 2)
            first_row = table_values(rtab[0:1, :], mybir.EngineType.SP, E * REGION + SPARE * P - P)
            sp.wait_ge(s_rows, 16 * NT)
            sp.wait_ge(s_pad, 16 * (E + 1))
            for j in range(CAP):
                if j >= 4:
                    sp.wait_ge(g_x[j % 4], 16 * (j // 4))
                sp.dma_start(xg[:, j, :], rows_dram[bass.ds(first_row[j], P), :]).then_inc(g_x[j % 4], 16)

        @block.gpsimd
        def _(pool):
            g = nc.gpsimd
            g.memset(ident[:, :], 0.0).then_inc(c_pool, 1)
            g.memset(before[:, :], 1.0).then_inc(c_pool, 1)
            pool.wait_ge(c_pool, 2)
            g.affine_select(out=ident[:, :], in_=ident[:, :], compare_op=ALU.not_equal, fill=1.0, base=0,
                            pattern=[[-1, P]], channel_multiplier=1).then_inc(c_pool, 1)
            g.affine_select(out=before[:, :], in_=before[:, :], compare_op=ALU.is_gt, fill=0.0, base=0,
                            pattern=[[1, P]], channel_multiplier=-1).then_inc(c_pool, 1)
            g.iota(tile_no[:, :], pattern=[[1, CAP]], base=0, channel_multiplier=0,
                   allow_small_or_imprecise_dtypes=True).then_inc(c_pool, 1)
            g.iota(tile_thr[:, :], pattern=[[P, NT]], base=0, channel_multiplier=0,
                   allow_small_or_imprecise_dtypes=True).then_inc(c_pool, 1)
            g.iota(first_wt[:, :], pattern=[[-1, E]], base=E, channel_multiplier=0,
                   allow_small_or_imprecise_dtypes=True).then_inc(c_pool, 1)
            g.iota(region0[:, :], pattern=[[REGION, E]], base=0, channel_multiplier=0,
                   allow_small_or_imprecise_dtypes=True).then_inc(c_pool, 1)
            g.iota(x1[:, :, ROW - 1].bitcast(i32), pattern=[[P, NT]], base=0, channel_multiplier=1)\
                .then_inc(c_pool, 1)
            g.memset(pad[:, :, 0:ROW - 1], 0.0).then_inc(c_pad, 1)
            g.iota(pad[:, :, ROW - 1].bitcast(i32), pattern=[[0, SPARE]], base=NOWHERE, channel_multiplier=0)\
                .then_inc(c_pad, 1)
            pool.wait_ge(l_b2, 16)
            g.tensor_scalar(b2r[:, 0, :], b2[:, :], S, 1.0, ALU.mult, ALU.mult).then_inc(p_b2, 1)
            pool.wait_ge(p_b2, 1)
            g.tensor_copy(b2e[:, 0, :], b2r[:, 0, :]).then_inc(p_b2, 1)
            pool.wait_ge(p_b2, 2)
            g.tensor_tensor(b2r[:, 1, :], b2r[:, 0, :], b2e[:, 0, :], ALU.subtract).then_inc(p_b2, 1)
            pool.wait_ge(p_b2, 3)
            g.tensor_copy(b2e[:, 1, :], b2r[:, 1, :]).then_inc(p_b2, 1)
            pool.wait_ge(p_b2, 4)
            g.tensor_tensor(b2e[:, 2, :], b2r[:, 1, :], b2e[:, 1, :], ALU.subtract).then_inc(p_b2, 1)
            for gr in range(4):
                pool.wait_ge(a_mean, 4)
                pool.wait_ge(a_row, gr + 1)
                pool.wait_ge(r_pos, gr + 1)
                for k, t in enumerate(range(NT)[gtiles(gr)]):
                    g.indirect_dma_start(
                        out=rows_dram, out_offset=bass.IndirectOffsetOnAxis(
                            ap=pos[:, 4 * gr + k:4 * gr + k + 1].bitcast(u32), axis=0),
                        in_=x1[:, t, :], in_offset=None).then_inc(s_rows, 16)

            for j in range(CAP):
                if j < CAP - LAST:
                    pool.wait_ge(e_zn, j + 1)
                    g.tensor_tensor(o[:, j, :], zn[:, j % 2, :], xg[:, j, 0:D], ALU.add).then_inc(e_o, 1)
                wait_output(pool, j)
                g.indirect_dma_start(out=out_rows, out_offset=bass.IndirectOffsetOnAxis(
                                         ap=xg[:, j, ROW - 1:ROW].bitcast(u32), axis=0),
                                     in_=o[:, j, :], in_offset=None, bounds_check=T - 1, oob_is_err=False)\
                    .then_inc(s_out, 16)
            pool.wait_ge(s_out, 16 * CAP)

        @block.scalar
        def _(act):
            s = nc.scalar
            act.dma_start(cent[:, :], cent_d).then_inc(l_cent, 16)
            act.dma_start(wo[:, :], wo_d).then_inc(l_wo, 16)
            act.wait_ge(c_dve, 4)
            s.activation(warm[:, :], eps_t[:, 0:1], ACT.Sqrt, bias=eps_t[:, 0:1])

            def evac_T(n):
                dst = xT[:, 4 * n:4 * n + 4, :] if n < 4 else attT[:, n - 4, :, :]
                act.wait_ge(a_T, n + 1)
                s.activation(dst, bT[n % 2][:, :].rearrange("p (t c) -> p t c", c=P), ACT.Copy).then_inc(a_Te, 1)

            def sd_1(q):
                act.wait_ge(a_var, 4 * q + 4)
                s.activation(rs1[:, 4 * q:4 * q + 4], mv1[:, 4 * q:4 * q + 4, 1], ACT.Sqrt, bias=eps_t[:, 0:1])\
                    .then_inc(a_sd, 1)

            def values(n):
                act.wait_ge(a_v, n + 1)
                act.wait_ge(a_rs, 1)
                for k, t in enumerate((2 * n, 2 * n + 1)):
                    s.activation(v[:, t, :], pair(bV[n])[:, k, 0:D], ACT.Copy, scale=rs1[:, t:t + 1])
                s.activation(xc[:, 2 * n:2 * n + 2, :], pair(bV[n])[:, :, D:CE], ACT.Copy).then_inc(a_vs, 1)

            def evac_C(c):
                act.wait_ge(a_c, c + 1)
                s.activation(att[:, c, :, :], bC[c % 2][:, :].rearrange("p (b d) -> p b d", d=D), ACT.Copy)\
                    .then_inc(a_ce, 1)

            def o_stats(n):
                act.wait_ge(a_o, n + 1)
                for k, t in enumerate(otiles(n)):
                    s.activation(xg[:, t, 0:D], pair(bO[n % 4])[:, k, 0:D], ACT.Square, accum_out=ssq[:, t:t + 1])\
                        .then_inc(a_sq, 1)
                t0, t1 = otiles(n)
                act.wait_ge(a_sq, 2 * n + 2)
                s.activation(rso[:, t0:t1 + 1:2], ssq[:, t0:t1 + 1:2], ACT.Sqrt, bias=eps_t[:, 0:1], scale=1.0 / D)\
                    .then_inc(a_osd, 1)

            def x1_var(n):
                act.wait_ge(a_x1, 2 * n + 2)
                for k, t in enumerate(otiles(n)):
                    s.activation(o[:, t, :], x1[:, t, 0:D], ACT.Square, bias=mv1[:, t, 0:1], scale=-1.0,
                                 accum_out=ssq2[:, t:t + 1]).then_inc(a_var2, 1)

            def sd_2(gr):
                t0 = HALF * (gr // 2) + gr % 2
                act.wait_ge(a_var2, (2, 4, 8, 12)[gr])
                if gr < 2:
                    act.wait_ge(a_var2d, 2 * gr + 2)
                var = ssq2[:, t0:t0 + 7:2]
                s.activation(x1[:, t0:t0 + 7:2, D + 2], var, ACT.Sqrt, bias=eps_t[:, 1:2], scale=1.0 / (D * S ** 2))\
                    .then_inc(a_sd2, 1)
                s.activation(x1[:, t0:t0 + 7:2, D + 1], var, ACT.Sqrt, bias=eps_t[:, 2:3], scale=(1.0 + EPS) / D)\
                    .then_inc(a_sd2, 1)

            def w1_high(e):
                act.wait_ge(l_w1[e // 4], 16)
                act.wait_ge(p_gS, 1)
                s.activation(w1p[:, e, :, 0, :], w1[:, e, :].rearrange("p (f c) -> p f c", f=FB), ACT.Copy, scale=gS[:, e:e + 1])\
                    .then_inc(p_w1h, 1)

            evac_T(0)
            sd_1(0)
            evac_T(1)
            sd_1(1)
            values(0)
            values(1)
            evac_T(2)
            sd_1(2)
            evac_C(0)
            evac_T(3)
            w1_high(0)
            sd_1(3)
            evac_C(1)
            evac_T(4)
            evac_T(5)
            o_stats(0)
            o_stats(1)
            x1_var(0)
            evac_C(2)
            o_stats(2)
            sd_2(0)
            o_stats(3)
            evac_C(3)
            x1_var(2)
            evac_T(6)
            evac_T(7)
            o_stats(4)
            sd_2(1)
            o_stats(5)
            o_stats(6)
            x1_var(4)
            x1_var(5)
            sd_2(2)
            o_stats(7)
            x1_var(6)
            x1_var(7)
            sd_2(3)
            for e in range(1, E):
                w1_high(e)
            pad_experts(act, mybir.EngineType.Activation, range(E // 2, E))

            def high(j):
                act.wait_ge(e_xT, j + 1)
                if j >= 2:
                    act.wait_ge(e_h1b, j - 1)
                s.activation(xh[:, j % 2, :], psX[j % 2][:, 0:P], ACT.Copy).then_inc(e_xh, 1)

            def hidden_a(j):
                act.wait_ge(e_h1a, j + 1)
                if j >= 3:
                    act.wait_ge(e_y, j - 2)
                for f in range(3):
                    last = s.activation(h[:, j % 3, f, :], psHa[j % 2][:, f * P:(f + 1) * P], ACT.Relu,
                                        bias=b1s[:, bass.ds(expert[j] * FB + f, 1)])
                last.then_inc(e_ha, 1)

            def sd_3(j):
                act.wait_ge(e_var, j + 1)
                s.activation(sd3[:, j % 2:j % 2 + 1], mv3[:, j % 2, 1:2], ACT.Sqrt, bias=eps_t[:, 3:4])\
                    .then_inc(e_sd, 1)

            def normalised(j):
                act.wait_ge(e_nm, j + 1)
                if j >= 2:
                    wait_output(act, j - 2)
                s.activation(zn[:, j % 2, :], z[:, j % 2, :], ACT.Identity, scale=rs3[:, j % 2:j % 2 + 1],
                             bias=nm3[:, j % 2:j % 2 + 1]).then_inc(e_zn, 1)

            act.wait_ge(r_tab, 1)
            expert = table_values(etab[0:1, :], mybir.EngineType.Activation, E - 1)
            act.wait_ge(p_b1s, 1)
            high(0)
            for j in range(CAP + 3):
                if 1 <= j <= CAP:
                    hidden_a(j - 1)
                if j + 1 < CAP:
                    high(j + 1)
                if 4 <= j < CAP + 2:
                    normalised(j - 4)
                if 3 <= j < CAP + 3:
                    sd_3(j - 3)

        @block.vector
        def _(dve):
            d = nc.vector
            for k, value in enumerate((EPS, EPS / S ** 2, EPS ** 2, EPS * S ** 2)):
                d.memset(eps_t[:, k:k + 1], value).then_inc(c_dve, 1)
            d.memset(ones3[:, :], 1.0).then_inc(c_dve, 1)
            d.memset(ones_bf[:, :], 1.0).then_inc(c_dve, 1)
            d.memset(ones_e[:, :], 1.0).then_inc(c_dve, 1)
            d.memset(hot[:, :, :], 0.0).then_inc(c_dve, 1)

            def x_rstd(q):
                dve.wait_ge(a_sd, q + 1)
                d.reciprocal(rs1[:, 4 * q:4 * q + 4], rs1[:, 4 * q:4 * q + 4]).then_inc(a_rs, 1)
                dve.wait_ge(a_var, 4 * q + 4)
                d.tensor_copy(x1[:, 4 * q:4 * q + 4, D], mv1[:, 4 * q:4 * q + 4, 0]).then_inc(a_mean, 1)

            def x_stat(t):
                if t % 4 == 0:
                    dve.wait_ge(l_x[t // 4], 16)
                d.bn_stats(st1[:, t, :], x[:, t, :]).then_inc(a_st, 1)

            def x_var(q):
                for t in range(4 * q, 4 * q + 4):
                    dve.wait_ge(a_st, t + 1)
                    d.bn_aggr(mv1[:, t, :], st1[:, t, :]).then_inc(a_var, 1)

            dve.wait_ge(l_cent, 16)
            d.reduce_sum(csum[:, :], cent[:, :], AX.X).then_inc(p_cent, 1)
            x_stat(0)
            dve.wait_ge(p_cent, 1)
            d.tensor_scalar(csum[:, :], csum[:, :], -1.0 / D, None, ALU.mult).then_inc(p_cent, 1)
            x_stat(1)
            dve.wait_ge(p_cent, 2)
            d.tensor_scalar(cent[:, :], cent[:, :], csum[:, 0:1], None, ALU.add).then_inc(p_cent, 1)
            dve.wait_ge(l_wi, 16)
            d.reduce_sum(colsum[:, :], wi[:, :], AX.X).then_inc(p_wi, 1)
            x_stat(2)
            dve.wait_ge(p_wi, 1)
            d.tensor_scalar(colsum[:, :], colsum[:, :], -1.0 / D, None, ALU.mult).then_inc(p_wi, 1)
            x_stat(3)
            dve.wait_ge(p_wi, 2)
            d.tensor_scalar(wi[:, :], wi[:, :], colsum[:, 0:1], None, ALU.add).then_inc(p_wi, 1)
            dve.wait_ge(c_pool, 3)
            d.tensor_scalar(centring[:, 0:D], ident[:, :], -1.0 / D, None, ALU.add).then_inc(p_wo, 1)
            x_var(0)
            dve.wait_ge(p_T, 1)
            d.tensor_copy(wxc[:, D:CE], bank[7][:, 0:E]).then_inc(p_w, 1)
            d.tensor_copy(centring[:, D:CE], bank[7][:, 0:E]).then_inc(p_wo, 1)
            dve.wait_ge(p_T, 2)
            d.tensor_copy(wxc[:, 0:D], bank[6][:, 0:P]).then_inc(p_w, 1)

            def other_parameters():
                dve.wait_ge(p_T, 3)
                d.tensor_copy(woc[:, :], bank[6][:, 0:CE]).then_inc(p_woc, 1)
                dve.wait_ge(p_T, 4)
                d.tensor_copy(smallT[:, :], bank[7][:, 0:NR]).then_inc(p_smallT, 1)
                dve.wait_ge(p_smallT, 1)
                d.tensor_scalar(gS[:, :], smallT[:, 0:E], S, None, ALU.mult).then_inc(p_gS, 1)

            def values(n):
                dve.wait_ge(a_v, n + 1)
                t0 = 2 * n
                if n % 2 == 0:
                    dve.wait_ge(a_rs, n // 2 + 1)
                src = pair(bV[n])
                d.tensor_tensor(v[:, t0:t0 + 2, :], src[:, :, 0:D],
                                rs1[:, t0:t0 + 2].unsqueeze(2).broadcast_to([P, 2, D]), ALU.mult)
                d.tensor_copy(xc[:, t0:t0 + 2, :], src[:, :, D:CE]).then_inc(a_ve, 1)

            def row_rstd(gr):
                t0 = HALF * (gr // 2) + gr % 2
                dve.wait_ge(a_sd2, 2 * gr + 2)
                d.reciprocal(x1[:, t0:t0 + 7:2, D + 1:D + 3], x1[:, t0:t0 + 7:2, D + 1:D + 3]).then_inc(a_row, 1)

            def over_e(a):
                return a.unsqueeze(2).broadcast_to([P, GT, E])

            def over_t(a):
                return a.unsqueeze(1).broadcast_to([P, GT, E])

            def choose(gr, step):
                logit, k, m = lg[:, gtiles(gr), :], key[:, 4 * gr:4 * gr + 4, :], mx[:, 4 * gr:4 * gr + 4]
                if step:
                    dve.wait_ge(r_key, 4 * gr + step)
                if step == 0:
                    dve.wait_ge(a_lg, 2 * gr + 2)
                    d.reduce_max(m, logit, AX.X).then_inc(r_key, 1)
                elif step == 1:
                    d.tensor_tensor(k, logit, over_e(m), ALU.is_equal).then_inc(r_key, 1)
                elif step == 2:
                    d.tensor_tensor(k, k, over_t(first_wt[:, :]), ALU.mult).then_inc(r_key, 1)
                elif step == 3:
                    d.reduce_max(m, k, AX.X).then_inc(r_key, 1)
                else:
                    d.tensor_tensor(hot[:, gr, GT:2 * GT, :], k, over_e(m), ALU.is_equal).then_inc(r_hot, 1)

            def place(gr, step):
                f, m = posf[:, 4 * gr:4 * gr + 4, :], mx[:, 4 * gr:4 * gr + 4]
                if step == 4:
                    row_rstd(gr)
                if step >= 2:
                    dve.wait_ge(r_place, 4 * gr + step)
                if step == 0:
                    dve.wait_ge(r_rank, gr + 1)
                    if gr:
                        dve.wait_ge(r_place, 4 * gr - 2)
                    d.tensor_tensor(f, rank[:, 0:GT, :], over_t(base[:, gr, :]), ALU.add).then_inc(r_place, 1)
                elif step == 1:
                    d.tensor_tensor(base[:, gr + 1, :], rank[:, GT, :], base[:, gr, :], ALU.add).then_inc(r_place, 1)
                elif step == 2:
                    d.tensor_tensor(f, f, hot[:, gr, GT:2 * GT, :], ALU.mult).then_inc(r_place, 1)
                elif step == 3:
                    d.reduce_sum(m, f, AX.X).then_inc(r_place, 1)
                else:
                    d.tensor_copy(pos[:, 4 * gr:4 * gr + 4], m).then_inc(r_pos, 1)

            def no_route(step):
                pass

            def residual(n, route):
                t0, t1 = otiles(n)
                two = slice(t0, t1 + 1, 2)
                dve.wait_ge(a_osd, n + 1)
                d.reciprocal(rso[:, two], rso[:, two]).then_inc(a_ors, 1)
                route(0)
                dve.wait_ge(a_ors, n + 1)
                src = pair(bO[n % 4])
                route(1)
                d.tensor_tensor(ocr[:, two, :], src[:, :, D:CE], rso[:, two].unsqueeze(2).broadcast_to([P, 2, E]),
                                ALU.mult).then_inc(a_oe, 1)
                for k, t in enumerate((t0, t1)):
                    d.scalar_tensor_tensor(x1[:, t, 0:D], src[:, k, 0:D], rso[:, t:t + 1], x[:, t, :],
                                           ALU.mult, ALU.add).then_inc(a_x1, 1)
                    route(2 + k)
                dve.wait_ge(a_oe, n + 1)
                d.tensor_tensor(lg[:, two, :], ocr[:, two, :], xc[:, two, :], ALU.add).then_inc(a_lg, 1)
                route(4)

            def x1_var(n):
                dve.wait_ge(a_x1, 2 * n + 2)
                for k, t in enumerate(otiles(n)):
                    d.scalar_tensor_tensor(o[:, t, :], x1[:, t, 0:D], mv1[:, t, 0:1], x1[:, t, 0:D],
                                           ALU.subtract, ALU.mult, accum_out=ssq2[:, t:t + 1]).then_inc(a_var2d, 1)

            def x_stats(q):
                for t in range(4 * q, 4 * q + 4):
                    x_stat(t)
                x_var(q)

            def w1_low(e):
                dve.wait_ge(p_w1h, e + 1)
                d.scalar_tensor_tensor(w1p[:, e, :, 1, :], w1[:, e, :].rearrange("p (f c) -> p f c", f=FB),
                                       gS[:, e:e + 1], w1p[:, e, :, 0, :], ALU.mult, ALU.subtract).then_inc(p_w1l, 1)

            x_stat(4)
            x_stat(5)
            x_rstd(0)
            x_stat(6)
            x_stat(7)
            x_var(1)
            x_rstd(1)
            values(2)
            values(3)
            other_parameters()
            x_stats(2)
            x_stats(3)
            x_rstd(2)
            x_rstd(3)
            dve.wait_ge(c_pool, 9)
            dve.wait_ge(c_dve, 8)
            d.tensor_copy(base[:, 0, :], region0[:, :]).then_inc(r_dve, 1)
            w1_low(0)
            values(4)
            values(5)
            values(6)
            values(7)
            dve.wait_ge(a_vs, 2)
            residual(0, no_route)
            residual(1, no_route)
            dve.wait_ge(r_dve, 1)
            for step in range(5):
                choose(0, step)
            x1_var(1)
            for step in range(5):
                place(0, step)
            residual(2, no_route)
            residual(3, no_route)
            for step in range(5):
                choose(1, step)
            x1_var(3)
            for step in range(5):
                place(1, step)
            residual(4, no_route)
            residual(5, no_route)
            for step in range(5):
                choose(2, step)
            for step in range(5):
                place(2, step)
            residual(6, no_route)
            residual(7, no_route)
            for step in range(5):
                choose(3, step)
            for step in range(5):
                place(3, step)
            links = [1]

            def link(ins):
                links[0] += 1
                ins.then_inc(r_dve, 1)
                dve.wait_ge(r_dve, links[0])

            d.tensor_copy(free_i[:, :], base[0:1, 4, :]).then_inc(r_free, 1)
            link(d.tensor_tensor(count[:, :], base[0:1, 4, :], region0[0:1, :], ALU.subtract))
            link(d.tensor_tensor(cmpt[:, :, :], count[:, :].unsqueeze(2).broadcast_to([1, E, NT]),
                                 tile_thr[0:1, :].unsqueeze(1).broadcast_to([1, E, NT]), ALU.is_gt))
            link(d.reduce_sum(ntile[:, :], cmpt[:, :, :], AX.X))
            link(d.tensor_tensor_scan(tend[:, :], ones_e[0:1, :], ntile[:, :], 0.0, ALU.mult, ALU.add))
            link(d.tensor_tensor(past[:, :, :], tend[:, :].unsqueeze(1).broadcast_to([1, CAP, E]),
                                 tile_no[:, :].unsqueeze(2).broadcast_to([1, CAP, E]), ALU.is_le))
            link(d.reduce_sum(ef[:, :], past[:, :, :], AX.X))
            d.tensor_scalar(etab[:, :], ef[:, :], float(E - 1), None, ALU.min).then_inc(r_tab, 1)
            link(d.tensor_scalar(skip[:, :], ntile[:, :], -float(P), float(REGION), ALU.mult, ALU.add))
            link(d.tensor_tensor(jump[:, :, :], past[:, :, :], skip[:, :].unsqueeze(1).broadcast_to([1, CAP, E]),
                                 ALU.mult))
            link(d.reduce_sum(rf[:, :], jump[:, :, :], AX.X))
            d.scalar_tensor_tensor(rtab[:, :], tile_no[:, :], float(P), rf[:, :], ALU.mult, ALU.add)\
                .then_inc(r_tab, 1)
            for e in range(1, E):
                w1_low(e)
            dve.wait_ge(p_b1, E)
            link(d.tensor_tensor(b1s[:, :], b1_ps, smallT[:, 2 * E:NR], ALU.add))
            d.tensor_scalar(b1s[:, :], b1s[:, :], S, None, ALU.mult).then_inc(p_b1s, 1)

            def norm(j):
                dve.wait_ge(g_x[j % 4], 16 * (j // 4 + 1))
                if j >= 3:
                    dve.wait_ge(e_xT, j - 2)
                d.tensor_scalar(xn[:, j % 3, :], xg[:, j, 0:D], xg[:, j, D:D + 1], xg[:, j, D + 1:D + 2],
                                ALU.subtract, ALU.mult).then_inc(e_xn, 1)

            def low(j):
                dve.wait_ge(e_xh, j + 1)
                d.tensor_tensor(xl[:, j % 2, :], psX[j % 2][:, 0:P], xh[:, j % 2, :], ALU.subtract)\
                    .then_inc(e_xl, 1)

            def hidden_b(j):
                dve.wait_ge(e_h1b, j + 1)
                if j >= 3:
                    dve.wait_ge(e_y, j - 2)
                d.tensor_scalar(h[:, j % 3, 3, :], psHb[j % 2][:, 0:P], b1s[:, bass.ds(expert[j] * FB + 3, 1)], 0.0,
                                ALU.add, ALU.max).then_inc(e_hb, 1)

            def output_sum(j):
                dve.wait_ge(e_y, j + 1)
                if j >= 2:
                    dve.wait_ge(e_zn, j - 1)
                d.scalar_tensor_tensor(z[:, j % 2, :], xg[:, j, 0:D], xg[:, j, D + 2:D + 3], psY[j % 2][:, 0:D],
                                       ALU.mult, ALU.add).then_inc(e_z, 1)

            def output_stats(j):
                dve.wait_ge(e_z, j + 1)
                d.bn_stats(st3[:, j % 2, :], z[:, j % 2, :]).then_inc(e_st, 1)

            def output_var(j):
                dve.wait_ge(e_st, j + 1)
                d.bn_aggr(mv3[:, j % 2, :], st3[:, j % 2, :]).then_inc(e_var, 1)

            def output_rstd(j):
                dve.wait_ge(e_sd, j + 1)
                d.reciprocal(rs3[:, j % 2:j % 2 + 1], sd3[:, j % 2:j % 2 + 1]).then_inc(e_rs, 1)

            def output_shift(j):
                dve.wait_ge(e_rs, j + 1)
                d.tensor_scalar(nm3[:, j % 2:j % 2 + 1], mv3[:, j % 2, 0:1], rs3[:, j % 2:j % 2 + 1], -1.0,
                                ALU.mult, ALU.mult).then_inc(e_nm, 1)

            def last_normalised(j):
                dve.wait_ge(e_rs, j + 1)
                wait_output(dve, j - 2)
                d.tensor_scalar(zn[:, j % 2, :], z[:, j % 2, :], mv3[:, j % 2, 0:1], rs3[:, j % 2:j % 2 + 1],
                                ALU.subtract, ALU.mult).then_inc(e_zlast, 1)

            def output(j):
                if j < CAP - 2:
                    dve.wait_ge(e_zn, j + 1)
                else:
                    dve.wait_ge(e_zlast, j - (CAP - 2) + 1)
                d.tensor_tensor(o[:, j, :], zn[:, j % 2, :], xg[:, j, 0:D], ALU.add).then_inc(e_olast, 1)

            dve.wait_ge(r_tab, 1)
            expert = table_values(etab[0:1, :], mybir.EngineType.DVE, E - 1)
            norm(0)
            norm(1)
            low(0)
            for j in range(CAP + 2):
                if j >= 4:
                    output_rstd(j - 4)
                if j >= 3:
                    output_sum(j - 3)
                if j >= 4:
                    output_shift(j - 4)
                if j + 2 < CAP:
                    norm(j + 2)
                if j >= 3:
                    output_stats(j - 3)
                if 1 <= j <= CAP:
                    hidden_b(j - 1)
                if j >= 3:
                    output_var(j - 3)
                if j + 1 < CAP:
                    low(j + 1)
            output(CAP - 3)
            output_sum(CAP - 1)
            output_rstd(CAP - 2)
            output_stats(CAP - 1)
            last_normalised(CAP - 2)
            output_var(CAP - 1)
            output(CAP - 2)
            output_rstd(CAP - 1)
            last_normalised(CAP - 1)
            output(CAP - 1)

        @block.tensor
        def _(pe):
            t_ = nc.tensor

            def transposes(n, src, done):
                if n >= 2:
                    pe.wait_ge(a_Te, n - 1)
                for k in range(4):
                    last = t_.transpose(bT[n % 2][:, k * P:(k + 1) * P], src[k], ident[:, :])
                last.then_inc(done, 1)

            def x_T(q):
                pe.wait_ge(l_x[q], 16)
                transposes(q, [x[:, 4 * q + k, :] for k in range(4)], a_T)

            def att_T(n):
                pe.wait_ge(a_ce, n - 3)
                transposes(n, [att[:, n - 4, k, :] for k in range(4)], a_T)

            def project_x(n):
                if n % 2 == 0:
                    pe.wait_ge(a_Te, n // 2 + 1)
                if n >= 6:
                    pe.wait_ge(a_ve, n - 3)
                for k in range(2):
                    last = t_.matmul(pair(bV[n])[:, k, :], xT[:, 2 * n + k, :], wxc[:, :], start=True, stop=True)
                last.then_inc(a_v, 1)

            def attend(c, groups=range(NG)):
                hf, qb = c // 2, c % 2
                if c >= 2:
                    pe.wait_ge(a_ce, c - 1)
                dst = bC[c % 2][:, :].rearrange("p (b u g i) -> p b u g i", b=NB, u=2, g=NG)
                val = v[:, HALF * hf:HALF * (hf + 1), :].rearrange("p (b k) (u g i) -> p k b u g i", k=2, u=2, g=NG)
                for g in groups:
                    for kb in range(2):
                        off = P * (1 - kb + qb)
                        last = t_.matmul(dst[:, :, :, g, :], toep[:, g, off:off + P], val[:, kb, :, :, g, :],
                                         start=(kb == 0), stop=(kb == 1))
                if groups[-1] == NG - 1:
                    last.then_inc(a_c, 1)

            def project_o(n):
                if n % 2 == 0:
                    pe.wait_ge(a_Te, n // 2 + 5)
                if n >= 4:
                    pe.wait_ge(a_x1, 2 * (n - 3))
                    pe.wait_ge(a_oe, n - 3)
                elif n >= 2:
                    pe.wait_ge(a_ve, 6)
                for k in range(2):
                    last = t_.matmul(pair(bO[n % 4])[:, k, :], attT[:, n // 2, 2 * (n % 2) + k, :], woc[:, :],
                                     start=True, stop=True)
                last.then_inc(a_o, 1)

            def ln_b_w1(e):
                if e == 0:
                    pe.wait_ge(a_ce, 4)
                    pe.wait_ge(p_smallT, 1)
                pe.wait_ge(l_w1[e // 4], 16)
                for f in range(FB):
                    last = t_.matmul(b1_ps[:, e * FB + f:e * FB + f + 1], w1[:, e, f * P:(f + 1) * P],
                                     smallT[:, E + e:E + e + 1], start=True, stop=True)
                last.then_inc(p_b1, 1)

            def warm_up(products):
                for k in range(products):
                    t_.matmul(bank[5][:, 0:P], ident[:, :], ident[:, :], start=True, stop=True)

            pe.wait_ge(c_pool, 3)
            warm_up(4)
            x_T(0)
            warm_up(1)
            pe.wait_ge(p_cent, 3)
            t_.transpose(bank[7][:, 0:E], cent[:, :], ident[0:E, 0:E]).then_inc(p_T, 1)
            warm_up(1)
            pe.wait_ge(p_wi, 3)
            t_.transpose(bank[6][:, 0:P], wi[:, :], ident[:, :]).then_inc(p_T, 1)
            x_T(1)
            pe.wait_ge(p_w, 2)
            for n in range(4):
                project_x(n)
            pe.wait_ge(p_wo, 2)
            pe.wait_ge(l_wo, 16)
            t_.matmul(bank[6][:, 0:CE], wo[:, :], centring[:, :], start=True, stop=True).then_inc(p_T, 1)
            x_T(2)
            pe.wait_ge(l_small, 48)
            t_.transpose(bank[7][:, 0:NR], small[:, :], ident[0:NR, 0:NR]).then_inc(p_T, 1)
            pe.wait_ge(l_toep, 16)
            pe.wait_ge(a_ve, 2)
            pe.wait_ge(a_vs, 2)
            attend(0)
            x_T(3)
            attend(1)
            att_T(4)
            project_x(4)
            project_x(5)
            att_T(5)
            pe.wait_ge(p_woc, 1)
            pe.wait_ge(p_smallT, 1)
            project_o(0)
            project_x(6)
            project_x(7)
            project_o(1)

            def ranks(gr):
                pe.wait_ge(r_hot, gr + 1)
                if gr:
                    pe.wait_ge(r_pos, gr)
                    pe.wait_ge(a_Te, 7)
                else:
                    pe.wait_ge(c_pool, 4)
                    pe.wait_ge(c_dve, 8)
                for k in range(GT, 0, -1):
                    t_.matmul(rank[:, :, :], ones_bf[:, :], hot[:, gr, GT - k:2 * GT + 1 - k, :],
                              start=(k == GT), stop=False)
                t_.matmul(rank[:, :, :], before[:, :], hot[:, gr, GT:2 * GT + 1, :], start=False, stop=True)\
                    .then_inc(r_rank, 1)

            pe.wait_ge(a_ve, 6)
            attend(2)
            project_o(2)
            project_o(3)
            attend(3, range(NG // 4))
            ranks(0)
            attend(3, range(NG // 4, NG))
            pe.wait_ge(r_place, 2)
            att_T(6)
            att_T(7)
            project_o(4)
            ranks(1)
            for n in range(5, 8):
                project_o(n)
            ln_b_w1(0)
            ln_b_w1(1)
            ranks(2)
            ln_b_w1(2)
            ln_b_w1(3)
            ranks(3)
            for e in range(4, E):
                ln_b_w1(e)
            pe.wait_ge(a_ce, 4)
            warm_up(7)

            def input_T(j):
                pe.wait_ge(e_xn, j + 1)
                t_.transpose(psX[j % 2][:, 0:P], xn[:, j % 3, :], ident[:, :]).then_inc(e_xT, 1)

            def up(j, f):
                if f == 0:
                    pe.wait_ge(e_xl, j + 1)
                    if j >= 2:
                        pe.wait_ge(e_ha, j - 1)
                        pe.wait_ge(e_hb, j - 1)
                dst = (psHa[j % 2][:, f * P:(f + 1) * P] if f < 3 else psHb[j % 2][:, 0:P])
                w_high = of_expert(w1s, F, offset[j % 3], 4 * f * P, 2 * P).bitcast(f16)
                w_low = of_expert(w1s, F, offset[j % 3], 4 * f * P + 2 * P, 2 * P).bitcast(f16)
                t_.matmul(dst, w_high, xh[:, j % 2, :], start=True, stop=False)
                t_.matmul(dst, w_high, xl[:, j % 2, :], start=False, stop=False)
                last = t_.matmul(dst, w_low, xh[:, j % 2, :], start=False, stop=True)
                if f >= 2:
                    last.then_inc((e_h1a, e_h1b)[f - 2], 1)

            def bias(j):
                if j >= 2:
                    pe.wait_ge(e_z, j - 1)
                t_.matmul(psY[j % 2][:, 0:D], ones3[:, :], of_expert(b2p, F, offset[j % 3], 0, 2 * D).bitcast(bf16),
                          start=True, stop=False)

            def down(j, f):
                if f == 0 and j >= CAP - 2:
                    pe.wait_ge(e_ha, j + 1)
                    pe.wait_ge(e_hb, j + 1)
                w_block = of_expert(w2, FB * D, offset[j % 3], 4 * f * D, 4 * D).bitcast(fp32)
                product = t_.matmul(psY[j % 2][:, 0:D], h[:, j % 3, f, :], w_block, start=False, stop=(f == FB - 1))
                if f == FB - 1:
                    product.then_inc(e_y, 1)

            pe.wait_ge(r_tab, 1)
            expert = table_values(etab[0:1, :], mybir.EngineType.PE, E - 1)
            pe.wait_ge(p_w1l, E)
            pe.wait_ge(l_w2, 16)
            pe.wait_ge(l_b2p, 16)
            offset = [None] * 3
            input_T(0)
            for j in range(CAP + 2):
                if j + 1 < CAP:
                    input_T(j + 1)
                if j >= 2:
                    bias(j - 2)
                if j < CAP:
                    offset[j % 3] = pe.snap(expert[j] * (4 * F))
                for ups, downs in (((0, 1), (0, 1)), ((2, 3), (2, 3))):
                    for f in ups if j < CAP else ():
                        up(j, f)
                    for f in downs if j >= 2 else ():
                        down(j - 2, f)


_INS = ['L0_attn_values', 'L0_attn_input_weights', 'L0_attn_output_weight', 'L0_ffn_centroids', 'L0_ffn_ln_g',
        'L0_ffn_ln_b', 'L0_ffn_W1', 'L0_ffn_b1', 'L0_ffn_W2', 'L0_ffn_b2']


def toeplitz_table(np):
    dist = (np.arange(128)[:, None] - np.arange(384)[None, :] + 128).astype(np.float32)
    parts = []
    for std, off in zip(ATTN_STD, ATTN_OFFSET):
        std, off = np.float32(std), np.float32(off)
        norm = np.float32(1.0 / (float(std) * np.sqrt(2.0 * np.pi)))
        parts.append(norm * np.exp(np.float32(-0.5) * ((dist - off) / std) ** 2))
    return np.stack(parts, 1).reshape(128, -1).astype(np.float32)


def kernel(**inputs):
    import numpy as _np
    import concourse.bacc as _bacc
    from concourse import mybir as _mybir
    from concourse.bass_utils import run_bass_kernel_spmd as _run

    nc = _bacc.Bacc("TRN2", target_bir_lowering=False, num_devices=1)
    arrays, args = {}, []
    for name in _INS:
        a = _np.ascontiguousarray(inputs[name])
        arrays[f"in_{name}_dram"] = a
        args.append(nc.dram_tensor(f"in_{name}_dram", a.shape, _mybir.dt.from_np(a.dtype), kind="ExternalInput").ap())
    table = toeplitz_table(_np)
    arrays["in_toeplitz_dram"] = table
    args.append(nc.dram_tensor("in_toeplitz_dram", table.shape, _mybir.dt.float32, kind="ExternalInput").ap())
    shape = inputs['L0_attn_values'].shape
    args.append(nc.dram_tensor("out_0_dram", shape, _mybir.dt.float32, kind="ExternalOutput").ap())
    attention_moe_block(nc, *args)
    r = _run(nc, [arrays], core_ids=[0])
    return r.results[0]["out_0_dram"]
```
